# Optimizing a Trainium2 kernel written in Bass

```python
import numpy as np
import jax
import jax.numpy as jnp

def _softmax(x, axis=-1):
    return jax.nn.softmax(x, axis=axis)

def _gelu(x):
    return jax.nn.gelu(x, approximate=True)

def _silu(x):
    return jax.nn.silu(x)

def _sigmoid(x):
    return jax.nn.sigmoid(x)

def _layernorm(x, axis=-1, eps=1e-05):
    m = jnp.mean(x, axis=axis, keepdims=True)
    v = jnp.var(x, axis=axis, keepdims=True)
    return (x - m) / jnp.sqrt(v + eps)

def _scatter_add(tgt, idx, src, axis=0):
    return tgt.at[idx].add(src)

def _segment_sum(src, seg, n):
    return jax.ops.segment_sum(src, seg, n)
kernel_name = 'mk_seq_postln_d1_jaxref_r4_25c299'

def setup_inputs(seed: int=0):
    np.random.seed(seed)
    _w = jnp.asarray

    def _L0_attn_setup():
        import jax, jax.numpy as jnp
        import numpy as np
        EPS = 1.1920929e-07
        NUM_HEADS = 16
        SOFTCAP = 50.0

        def rms_norm(x):
            return x * jax.lax.rsqrt(jnp.mean(x * x, axis=-1, keepdims=True) + EPS)
        key = jax.random.key(seed)
        ks = jax.random.split(key, 5)
        B, S, D = (2, 512, 256)
        x = jax.random.normal(ks[0], (B, S, D), dtype=jnp.float32)
        w_q = jax.random.normal(ks[1], (D, D), dtype=jnp.float32) * 0.02
        w_k = jax.random.normal(ks[2], (D, D), dtype=jnp.float32) * 0.02
        w_v = jax.random.normal(ks[3], (D, D), dtype=jnp.float32) * 0.02
        w_o = jax.random.normal(ks[4], (D, D), dtype=jnp.float32) * 0.02
        return {'x': x, 'w_q': w_q, 'w_k': w_k, 'w_v': w_v, 'w_o': w_o}
    _L0_attn_in = _L0_attn_setup()

    def _L0_ffn_setup():
        import jax, jax.numpy as jnp
        import numpy as np
        EMB = 256
        FF = 4 * EMB

        def _ternary(w):
            scale = jnp.maximum(jnp.mean(jnp.abs(w)), 1e-08)
            w_t = jnp.clip(jnp.round(w / scale), -1.0, 1.0)
            return w + jax.lax.stop_gradient(w_t - w)
        key = jax.random.key(seed)
        kx, k1, k2, kb1, kb2 = jax.random.split(key, 5)
        x = jax.random.normal(kx, (4, 512, EMB), dtype=jnp.float32)
        lim1 = 1.0 / np.sqrt(EMB)
        lim2 = 1.0 / np.sqrt(FF)
        W1 = jax.random.uniform(k1, (FF, EMB), jnp.float32, -lim1, lim1)
        b1 = jax.random.uniform(kb1, (FF,), jnp.float32, -lim1, lim1)
        W2 = jax.random.uniform(k2, (EMB, FF), jnp.float32, -lim2, lim2)
        b2 = jax.random.uniform(kb2, (EMB,), jnp.float32, -lim2, lim2)
        return {'x': x, 'W1': W1, 'b1': b1, 'W2': W2, 'b2': b2}
    _L0_ffn_in = _L0_ffn_setup()
    _d = {'L0_attn_x': _L0_attn_in['x'], 'L0_attn_w_q': _L0_attn_in['w_q'], 'L0_attn_w_k': _L0_attn_in['w_k'], 'L0_attn_w_v': _L0_attn_in['w_v'], 'L0_attn_w_o': _L0_attn_in['w_o'], 'L0_ffn_W1': _L0_ffn_in['W1'], 'L0_ffn_b1': _L0_ffn_in['b1'], 'L0_ffn_W2': _L0_ffn_in['W2'], 'L0_ffn_b2': _L0_ffn_in['b2']}
    _x0 = _d['L0_attn_x']
    _d['L0_attn_x'] = jax.random.normal(jax.random.fold_in(jax.random.key(seed), 1), (4, 1024, 256), dtype=_x0.dtype)
    del _x0
    return _d

def reference(L0_attn_x, L0_attn_w_q, L0_attn_w_k, L0_attn_w_v, L0_attn_w_o, L0_ffn_W1, L0_ffn_b1, L0_ffn_W2, L0_ffn_b2):

    def _L0_attn_ref(x, w_q, w_k, w_v, w_o):
        import jax, jax.numpy as jnp
        import numpy as np
        EPS = 1.1920929e-07
        NUM_HEADS = 16
        SOFTCAP = 50.0

        def rms_norm(x):
            return x * jax.lax.rsqrt(jnp.mean(x * x, axis=-1, keepdims=True) + EPS)
        B, S, D = x.shape
        H = NUM_HEADS
        dk = D // H

        def split_heads(y):
            return y.reshape(B, S, H, dk).transpose(0, 2, 1, 3)
        q = split_heads(x @ w_q.T)
        k = split_heads(x @ w_k.T)
        v = split_heads(x @ w_v.T)
        q = rms_norm(q)
        k = rms_norm(k)
        scores = jnp.einsum('bhqd,bhkd->bhqk', q, k) / jnp.sqrt(jnp.float32(dk))
        scores = jnp.tanh(scores / SOFTCAP) * SOFTCAP
        causal = jnp.tril(jnp.ones((S, S), dtype=bool))
        scores = jnp.where(causal[None, None], scores, -jnp.inf)
        probs = jax.nn.softmax(scores, axis=-1)
        y = jnp.einsum('bhqk,bhkd->bhqd', probs, v)
        y = y.transpose(0, 2, 1, 3).reshape(B, S, D)
        return y @ w_o.T

    def _L0_ffn_ref(x, W1, b1, W2, b2):
        import jax, jax.numpy as jnp
        import numpy as np
        EMB = 256
        FF = 4 * EMB

        def _ternary(w):
            scale = jnp.maximum(jnp.mean(jnp.abs(w)), 1e-08)
            w_t = jnp.clip(jnp.round(w / scale), -1.0, 1.0)
            return w + jax.lax.stop_gradient(w_t - w)
        h = jnp.einsum('bsd,fd->bsf', x, _ternary(W1)) + b1
        h = jax.nn.gelu(h, approximate=False)
        out = jnp.einsum('bsf,df->bsd', h, _ternary(W2)) + b2
        return out
    x = L0_attn_x
    x = _layernorm(x + _L0_attn_ref(x, L0_attn_w_q, L0_attn_w_k, L0_attn_w_v, L0_attn_w_o), axis=-1)
    x = _layernorm(x + _L0_ffn_ref(x, L0_ffn_W1, L0_ffn_b1, L0_ffn_W2, L0_ffn_b2), axis=-1)
    return x

_drawn_inputs = setup_inputs


def setup_inputs(seed=0):
    import zlib

    import numpy as np

    out = dict(_drawn_inputs(seed))
    spreads = {}
    factors = {'L0_attn_w_q': 5.643,
     'L0_attn_w_k': 5.554,
     'L0_attn_w_v': 4.208,
     'L0_attn_w_o': 4.227,
     'L0_ffn_b1': 23.418,
     'L0_ffn_b2': 64.0}
    for name, (base, spread) in spreads.items():
        noise = np.random.default_rng([zlib.crc32(name.encode()), seed]).standard_normal(out[name].shape)
        drawn = base * np.exp(spread * noise) if base else spread * noise
        out[name] = jnp.asarray(drawn.astype(out[name].dtype))
    for name, factor in factors.items():
        out[name] = (out[name] * factor).astype(out[name].dtype)
    return out
```

```python
from contextlib import ExitStack

import concourse.bass as bass
from concourse import mybir

FP32, FP16, INT32 = mybir.dt.float32, mybir.dt.float16, mybir.dt.int32
ACT = mybir.ActivationFunctionType
ALU = mybir.AluOpType
AX = mybir.AxisListType

BATCH, SEQ, DIM = 4, 1024, 256
HEADS, HEAD_DIM, FF = 16, 16, 1024
SOFTCAP = 50.0
RMS_EPS, LN_EPS = 1.1920929e-07, 1e-05
P = 128
TILES = SEQ // P
CHUNK = 512
CT = CHUNK // P
GROUP_HEADS = 4
HGS = HEADS // GROUP_HEADS
UNITS = 2 * HGS
KT = DIM // P
FT = FF // P
GROUP = 1024
SIDE_BANKS = 3

def steps_of(half):
    steps = []
    for kt in range(CT * half):
        steps.append(([[(h, kt, (h % 2) * 512, 512, 0) for h in (2 * g, 2 * g + 1)] for g in range(2)], None))
    d = CT * half
    steps.append(([[(h, d, (h % 2) * 512, 512, 0) for h in (2 * g, 2 * g + 1)] for g in range(2)],
                  (2, 512, 1, 0)))
    steps.append(([[x for h in (2 * g, 2 * g + 1) for x in ((h, d + 1, (h % 2) * 512, 384, 128),
                                                           (h, d + 3, (h % 2) * 512 + 384, 128, 384))]
                   for g in range(2)], (2, 512, 2, 384)))
    steps.append(([[(h, d + 2, (h % 2) * 512 + (h // 2) * 256, 256, 256) for h in range(4)]], (4, 256, 1, 0)))
    return steps


STEPS = [steps_of(0), steps_of(1)]
UNIT_STEPS = [len(s) for s in STEPS]
UNIT_GROUPS = [sum(len(g) for g, _ in s) for s in STEPS]
UNIT_MASKS = [sum(len(g) for g, m in s if m) for s in STEPS]


def before_unit(per_half, u):
    return sum(per_half[v // HGS] if v < UNITS else 0 for v in range(u)) if u < UNITS else HGS * sum(per_half)


BATCH_STEPS, BATCH_GROUPS, BATCH_MASKS = (HGS * sum(x) for x in (UNIT_STEPS, UNIT_GROUPS, UNIT_MASKS))

SIDE_JOBS = ("fin", "prep_q", "prep_k", "xt", "qk", "v", "yt", "wo", "x1t", "f1", "f2")


def plan(kind):
    out = []
    if kind == "end":
        out += [("gelu", 0, -1), ("fin", UNITS - 1, -1)]
        for t in range(CT):
            out += [("yt", 1, t, -1), ("f2", 0, t, -1), ("wo", 1, t, -1), ("x1t", 1, t, -1),
                    ("f1", 1, t, -1, 0), ("f1", 1, t, -1, 1)]
        out += [("gelu", 1, -1)] + [("f2", 1, t, -1) for t in range(CT)]
        return out
    for u in range(UNITS):
        half, hg = divmod(u, HGS)
        n = UNIT_STEPS[half]
        slots = {(s, w): [] for s in range(n) for w in (0, 1)}
        post1 = None if kind == "first" and half == 0 else (1 - half, hg, -1 if half == 0 else 0)
        post2 = None if kind == "first" else (half, hg, -1)
        if kind == "first" and half == 1:
            post2 = None
        if hg == 0 and post2:
            out.append(("gelu", half, -1))
        if not (kind == "first" and u == 0):
            slots[0, 0].append(("fin", u - 1, 0) if u else ("fin", UNITS - 1, -1))
        nxt = [] if kind == "last" and u == UNITS - 1 else [("prep_q", u + 1)]
        if nxt:
            nxt.append(("prep_k", u + 1, 0))
            if HGS <= u + 1 < UNITS:
                nxt.append(("prep_k", u + 1, 1))
        pair = None
        if half == 1 and kind != "last":
            pair = (hg, 1)
        if half == 0 and kind == "first" and hg < 2:
            pair = (2 + hg, 0)
        if half == 0:
            if post1:
                slots[0, 0].append(("yt", *post1))
                slots[1, 0].append(("wo", *post1))
                slots[2, 0].append(("x1t", *post1))
                slots[2, 1] += [("f1", *post1, a) for a in (0, 1)]
            slots[0, 0] += nxt[:1]
            slots[1, 0] += nxt[1:]
            if post2:
                slots[1, 0].append(("f2", *post2))
            if pair:
                slots[0, 0] += [("xt", *pair, 0), ("xt", *pair, 1)]
                slots[1, 0] += [(k, *pair, t) for t in (0, 1) for k in ("qk", "v")] + [("norm", *pair)]
        else:
            slots[0, 0].append(("yt", *post1))
            slots[1, 0].append(("wo", *post1))
            if pair:
                slots[1, 0] += [("xt", *pair, 0), ("xt", *pair, 1)]
                slots[2, 0] += [("qk", *pair, 0), ("v", *pair, 0)]
                slots[3, 0] += [("qk", *pair, 1), ("v", *pair, 1), ("norm", *pair)]
            if post2:
                slots[2, 0].append(("f2", *post2))
            slots[4, 0] += [("x1t", *post1)] + nxt[:1]
            slots[5, 0] += nxt[1:] + [("f1", *post1, 0)]
            slots[5, 1] += [("f1", *post1, 1)]
        for s in range(n):
            if s + 1 < n:
                out.append(("scores", u, s + 1))
            elif not (kind == "last" and u == UNITS - 1):
                out.append(("scores", u + 1, 0))
            out += slots[s, 0]
            out.append(("attend", u, s))
            out += slots[s, 1]
    return out


PLANS = {k: plan(k) for k in ("first", "middle", "last", "end")}
PROLOGUE = ([x for p in (0, 1) for x in (("xt", p, 0, 0), ("xt", p, 0, 1), ("qk", p, 0, 0), ("v", p, 0, 0),
                                         ("qk", p, 0, 1), ("v", p, 0, 1), ("norm", p, 0))]
            + [("prep_q", 0), ("prep_k", 0, 0), ("scores", 0, 0)])
LINKS = {"fin": 1, "norm": 14, "wo": 4, "f2": 2}
PAIRS = TILES // 2


def kind_of(b):
    return {0: "first", BATCH - 1: "last", BATCH: "end"}.get(b, "middle") if isinstance(b, int) else "middle"


def counted(events, weigh):
    return sum(weigh(e) for e in events)


class Count:

    def __init__(self, weigh):
        self.weigh = weigh
        self.prologue = counted(PROLOGUE, weigh)
        self.first = counted(PLANS["first"], weigh)
        self.middle = counted(PLANS["middle"], weigh)
        self.last = counted(PLANS["last"], weigh)

    def batch(self, b):
        if isinstance(b, int):
            done = [0, self.first]
            for _ in range(1, BATCH - 1):
                done.append(done[-1] + self.middle)
            done.append(done[-1] + self.last)
            return self.prologue + done[b]
        return b * self.middle + (self.prologue + self.first - self.middle)

    def before(self, b, i):
        return self.batch(b) + counted(PLANS[kind_of(b)][:i], self.weigh)


def of(*names):
    return lambda e: int(e[0] in names)


SIDE = Count(of(*SIDE_JOBS))
LINK = Count(lambda e: LINKS.get(e[0], 0))
PAIR = Count(of("norm"))
GELUS = Count(of("gelu"))
LN = Count(of("wo", "f2"))
OUTS = Count(of("f2"))
WOS = Count(of("wo"))


def build(nc, x, w_q, w_k, w_v, w_o, W1, b1, W2, b2, out):
    x_t = x.rearrange("b (t p) d -> p (b t) d", p=P)
    out_t = out.rearrange("b (t p) d -> p (b t) d", p=P)
    ctx = ExitStack()
    with ctx:
        def sb(name, shape, dt=FP32):
            return ctx.enter_context(nc.sbuf_tensor(name, shape, dt))

        def sem(name):
            return ctx.enter_context(nc.semaphore(name))

        w_qkvT = sb("w_qkvT", [P, KT, 3 * DIM])
        w_oT = sb("w_oT", [P, KT, DIM])
        w1T = sb("w1T", [P, KT, FF], FP16)
        w2T = sb("w2T", [P, FT, DIM])
        b1_col = sb("b1_col", [P, FT])
        b2_row = sb("b2_row", [1, DIM])
        b2_all = sb("b2_all", [P, DIM])
        ident = sb("ident", [P, P])
        ident16 = sb("ident16", [P, P], FP16)
        ones = sb("ones", [P, P])
        minus_half = sb("minus_half", [P, 1])
        tern = sb("tern", [P, 2, 4])
        x_in = sb("x_in", [P, 2, 2, DIM])
        xT = sb("xT", [P, 2, KT, P])
        qk_raw = sb("qk_raw", [P, 2, 2 * DIM])
        qk_norm = sb("qk_norm", [P, 2, 2 * DIM])
        ssq = sb("ssq", [P, 64])
        rms = sb("rms", [P, 2, 64])
        newton = sb("newton", [P, 64])
        qk_parts = sb("qk_parts", [P, 2, 2 * TILES, HEADS, 4 * HEAD_DIM], FP16)
        values = sb("values", [P, 2 * TILES, DIM])
        qT = sb("qT", [P, 2, 2, CHUNK], FP16)
        kT = sb("kT", [P, 2, 2, 2, CHUNK], FP16)
        v_unit = sb("v_unit", [P, 2, TILES, GROUP_HEADS, 2 * HEAD_DIM])
        capped = sb("capped", [P, 2, GROUP])
        probs = sb("probs", [P, 2, 2, GROUP])
        yT_unit = sb("yT_unit", [P, CHUNK])
        inv_den = sb("inv_den", [P, CT * GROUP_HEADS])
        y_tok = sb("y_tok", [P, 2, CT, DIM])
        yT = sb("yT", [P, KT, P])
        x_res = sb("x_res", [P, 2, DIM])
        z = sb("z", [P, 3, DIM])
        stats = sb("stats", [P, 6])
        mean_var = sb("mean_var", [P, 2])
        var_eps = sb("var_eps", [P, 1])
        inv_std = sb("inv_std", [P, 1])
        x1 = sb("x1", [P, DIM])
        x1_parts = sb("x1_parts", [P, 2, DIM], FP16)
        x1_b2 = sb("x1_b2", [P, 2, CT, DIM])
        x1T = sb("x1T", [P, 2, KT, P], FP16)
        hidden = sb("hidden", [P, CT, FT, P])
        y_out = sb("y_out", [P, 2, DIM])
        w_in = capped[:, :, :].rearrange("p a (w k d) -> p (a w) k d", k=KT, d=DIM)
        room = hidden[:, :, :, :].rearrange("p t f c -> p (t f c)")
        room2 = probs[:, :, :, :].rearrange("p a g c -> p (a g c)")
        w1_in = room[:, 0:FF * KT].rearrange("p (f d) -> p f d", d=DIM)
        w2_in = room[:, FF * KT:2 * FF * KT].rearrange("p (o f) -> p o f", f=FF)
        w_neg = room2[:, 0:FF * KT]
        w2_tern = room2[:, FF * KT:2 * FF * KT].rearrange("p (o f) -> p o f", f=FF)
        w1_tern = x1_b2[:, :, :, :].rearrange("p a t d -> p (a t d)").bitcast(FP16)[:, 0:FF * KT]\
            .rearrange("p (f d) -> p f d", d=DIM)

        scores = ctx.enter_context(nc.psum_tensor("scores", [P, 2, GROUP], FP32))
        attended = ctx.enter_context(nc.psum_tensor("attended", [P, CHUNK], FP32))
        side = [ctx.enter_context(nc.psum_tensor(f"side{i}", [P, 512], FP32)) for i in range(SIDE_BANKS)]

        w_loaded = sem("w_loaded")
        w1_loaded = sem("w1_loaded")
        w2_loaded = sem("w2_loaded")
        bias_loaded = sem("bias_loaded")
        x_loaded = [sem("x_loaded0"), sem("x_loaded1")]
        res_loaded = [sem("res_loaded0"), sem("res_loaded1")]
        y_out_free = [sem("y_out_free0"), sem("y_out_free1")]
        consts = sem("consts")
        consts_step = sem("consts_step")
        setup_filled = sem("setup_filled")
        setup_drained = sem("setup_drained")
        ternary = sem("ternary")
        side_filled = sem("side_filled")
        side_drained = sem("side_drained")
        linked = sem("linked")
        high_ready = sem("high_ready")
        parts_ready = sem("parts_ready")
        v_staged = sem("v_staged")
        scores_ready = sem("scores_ready")
        capped_ready = sem("capped_ready")
        probs_ready = sem("probs_ready")
        masked = sem("masked")
        attend_done = sem("attend_done")
        yT_copied = sem("yT_copied")
        var_ready = sem("var_ready")
        inv_std_ready = sem("inv_std_ready")
        x1_ready = sem("x1_ready")
        x1_b2_ready = sem("x1_b2_ready")
        gelu_done = sem("gelu_done")
        out_ready = sem("out_ready")
        held = [sem(f"held{n}") for n in range(3)]

        block = ctx.enter_context(nc.Block())

        def batches(eng, emit):
            for i, e in enumerate(PLANS["first"]):
                emit(0, i, e)
            with eng.Fori(1, BATCH - 1) as b:
                for i, e in enumerate(PLANS["middle"]):
                    emit(b, i, e)
            for i, e in enumerate(PLANS["last"]):
                emit(BATCH - 1, i, e)
            for i, e in enumerate(PLANS["end"]):
                emit(BATCH, i, e)

        def hold(eng, semaphore, value):
            eng.wait_ge(semaphore, value)
            if not isinstance(value, int):
                eng.sem_inc(held[eng is nc.vector and 0 or eng is nc.tensor and 1 or 2], 1)

        def tiles_at(b, first, n):
            return bass.ds(b * TILES + first, n)

        def kept_at(b, first, n):
            at = (b & 1) * TILES + first
            return slice(at, at + n) if isinstance(at, int) else bass.ds(at, n)

        def part_slots(b, t, which):
            tile = qk_parts[:, which, kept_at(b, t, 1)].rearrange("p a h c -> p (a h) c")
            if which == 0:
                slots = tile.rearrange("p h (r k d) -> p h r k d", r=2, k=2)
                return slots[:, :, :, 0, :], slots[:, :, :, 1, :]
            slots = tile.rearrange("p h (k r d) -> p h k r d", r=2, k=2)
            return slots[:, :, 0, :, :], slots[:, :, 1, :, :]

        def head_view(t, which):
            return qk_norm[:, t, which * DIM:(which + 1) * DIM].rearrange("p (h d) -> p h d", d=HEAD_DIM)\
                .unsqueeze(2).to_broadcast([P, HEADS, 2, HEAD_DIM])

        def group_index(b, u, s, g):
            half = min(u, UNITS - 1) // HGS if u < UNITS else 0
            in_unit = sum(len(x) for x, _ in STEPS[half][:s]) + g
            return b * BATCH_GROUPS + before_unit(UNIT_GROUPS, u) + in_unit

        def step_index(b, u, s):
            return b * BATCH_STEPS + before_unit(UNIT_STEPS, u) + s

        def step_parity(u, s):
            return (before_unit(UNIT_STEPS, u % UNITS) + s) % 2

        def last_in_buffer(b, u, s, g):
            if isinstance(b, int) and b == 0 and u == 0 and s == 0:
                return None
            back, uu, ss = 0, u, s
            while True:
                ss -= 1
                if ss < 0:
                    uu -= 1
                    if uu < 0:
                        uu, back = UNITS - 1, 1
                    ss = UNIT_STEPS[unit_half(uu)] - 1
                if len(STEPS[unit_half(uu)][ss][0]) > g:
                    return group_index(b - back, uu, ss, g) + 1

        def unit_half(u):
            return (u % UNITS) // HGS

        @block.sync
        def _(sp):
            def load_pair(b, pair):
                sp.dma_start(x_in[:, pair % 2], x_t[:, tiles_at(b, 2 * pair, 2), :]).then_inc(x_loaded[pair % 2], 16)

            def load_residual(b, half, t):
                sp.dma_start(x_res[:, t % 2], x_t[:, b * TILES + CT * half + t, :] if isinstance(b, int)
                             else x_t[:, bass.ds(b * TILES + CT * half + t, 1), :].rearrange("p a d -> p (a d)"))\
                    .then_inc(res_loaded[t % 2], 16)

            for i, w in enumerate((w_q, w_k, w_v)):
                sp.dma_start(w_in[:, i], w.rearrange("(o p) d -> p o d", p=P)).then_inc(w_loaded, 16)
            sp.dma_start(w_in[:, 3], w_o.rearrange("(o p) d -> p o d", p=P)).then_inc(w_loaded, 16)
            load_pair(0, 0)
            load_pair(0, 1)
            sp.dma_start(w1_in[:, :, :], W1.rearrange("(f p) d -> p f d", p=P)).then_inc(w1_loaded, 16)
            sp.dma_start(w2_in[:, :, :], W2.rearrange("(o p) f -> p o f", p=P)).then_inc(w2_loaded, 16)
            sp.dma_start(b2_row[0:1, :], b2.rearrange("(a d) -> a d", a=1)).then_inc(bias_loaded, 16)
            with nc.allow_non_contiguous_dma(reason="1024 biases, once"):
                sp.dma_start(b1_col[:, :], b1.rearrange("(f p) -> p f", p=P)).then_inc(bias_loaded, 16)
            load_residual(0, 0, 0)
            load_residual(0, 0, 1)
            for p in (0, 1):
                sp.wait_ge(side_drained, 2 + 6 * p)
                load_pair(0, p + 2)

            def emit(b, i, e):
                if e[0] == "xt" and e[3] == 1:
                    pair, ahead = e[1], e[2]
                    if ahead == 0 or pair + 2 < PAIRS:
                        sp.wait_ge(side_drained, SIDE.before(b, i) + 1)
                        load_pair(b + 1, pair - 2 if ahead == 0 else pair + 2)
                if i == 0 and kind_of(b) == "middle":
                    sp.wait_ge(side_drained, SIDE.batch(b))
                    load_pair(b + 1, 0)
                    load_pair(b + 1, 1)
                if e[0] == "wo":
                    _, half, t, back = e
                    sp.wait_ge(side_drained, SIDE.before(b, i) + 1)
                    nb = b + back
                    if t + 2 < CT:
                        load_residual(nb, half, t + 2)
                    elif half == 0:
                        load_residual(nb, 1, t - 2)
                    elif not (isinstance(b, int) and b == BATCH):
                        load_residual(nb + 1, 0, t - 2)
                if e[0] == "f2":
                    _, half, t, back = e
                    sp.wait_ge(out_ready, OUTS.before(b, i) + 1)
                    nb = b + back
                    dst = out_t[:, bass.ds(nb * TILES + CT * half + t, 1), :].rearrange("p a d -> p (a d)") \
                        if not isinstance(nb, int) else out_t[:, nb * TILES + CT * half + t, :]
                    sp.dma_start(dst, y_out[:, t % 2]).then_inc(y_out_free[t % 2], 16)

            for par in range(2):
                sp.sem_inc(y_out_free[par], 16)
            batches(sp, emit)
            for par in range(2):
                sp.wait_ge(y_out_free[par], 16 + 16 * BATCH * TILES // 2)

        @block.gpsimd
        def _(pool):
            pool.memset(ident[:, :], 0.0).then_inc(consts_step, 1)
            pool.memset(ident16[:, :], 0.0).then_inc(consts_step, 1)
            pool.wait_ge(consts_step, 2)
            for m in (ident, ident16):
                pool.affine_select(out=m[:, :], in_=m[:, :], compare_op=ALU.not_equal, fill=1.0, base=0,
                                   pattern=[[-1, P]], channel_multiplier=1).then_inc(consts, 1)
            pool.memset(ones[:, :], 1.0).then_inc(consts, 1)
            pool.memset(minus_half[:, :], -0.5).then_inc(consts, 1)
            pool.memset(v_unit[:, :, :, :, HEAD_DIM:], 1.0).then_inc(consts, 1)
            pool.wait_ge(consts, 5)

            def low_parts(b, i, pair, ahead, wait):
                pool.wait_ge(high_ready, wait)
                for t in range(2):
                    for which in range(2):
                        high, low = part_slots(b + ahead, 2 * pair + t, which)
                        ins = pool.tensor_tensor(low, head_view(t, which), high, ALU.subtract)
                ins.then_inc(parts_ready, 1)

            def stage_values(b, u):
                n = TILES if unit_half(u) else CT
                hg = u % HGS
                bb = b + u // UNITS
                src = values[:, kept_at(bb, 0, n), GROUP_HEADS * HEAD_DIM * hg:GROUP_HEADS * HEAD_DIM * (hg + 1)]
                pool.tensor_copy(v_unit[:, u % 2, 0:n, :, 0:HEAD_DIM],
                                 src.rearrange("p t (h d) -> p t h d", d=HEAD_DIM)).then_inc(v_staged, 1)

            for p in (0, 1):
                low_parts(0, None, p, 0, p + 1)
            pool.wait_ge(side_drained, 12)
            stage_values(0, 0)

            def emit(b, i, e):
                if e[0] == "norm":
                    low_parts(b, i, e[1], e[2], PAIR.before(b, i) + 1)
                elif e[0] == "prep_q":
                    u = e[1]
                    pool.wait_ge(side_drained, SIDE.before(b, i))
                    if not (isinstance(b, int) and b == 0 and u < 2):
                        hold(pool, attend_done, step_index(b, u - 1, 0))
                    stage_values(b, u)
                elif e[0] in ("wo", "f2"):
                    pool.wait_ge(var_ready, LN.before(b, i) + 1)
                    pool.tensor_tensor(inv_std[:, :], var_eps[:, :], minus_half[:, :], ALU.pow)\
                        .then_inc(inv_std_ready, 1)
                    if e[0] == "wo":
                        _, half, t, _ = e
                        pool.wait_ge(x1_ready, WOS.before(b, i) + 1)
                        pool.tensor_tensor(x1_b2[:, half, t, :], x1[:, :], b2_all[:, :], ALU.add)\
                            .then_inc(x1_b2_ready, 1)
                elif e[0] == "attend":
                    _, u, s = e
                    groups, diag = STEPS[unit_half(u)][s]
                    if diag:
                        n, stride, m, inner = diag
                        for g in range(len(groups)):
                            hold(pool, probs_ready, group_index(b, u, s, g) + 1)
                            buf = probs[:, step_parity(u, s), g, :]
                            for k in range(m):
                                view = buf.rearrange("p (h c) -> p h c", c=stride)[:, :, k * inner:k * inner + P]
                                ins = pool.affine_select(out=view, in_=view, compare_op=ALU.is_ge, fill=0.0,
                                                         base=0, pattern=[[0, n], [1, P]], channel_multiplier=-1)
                            ins.then_inc(masked, 1)

            batches(pool, emit)

        @block.scalar
        def _(act):
            def emit(b, i, e):
                if e[0] == "attend":
                    _, u, s = e
                    groups, _ = STEPS[unit_half(u)][s]
                    for g in range(len(groups)):
                        n = group_index(b, u, s, g)
                        prev = last_in_buffer(b, u, s, g)
                        if prev is not None:
                            act.wait_ge(probs_ready, prev)
                        act.wait_ge(scores_ready, n + 1)
                        act.activation(capped[:, g, :], scores[:, g, :], ACT.Tanh,
                                       scale=1.0 / (SOFTCAP * HEAD_DIM ** 0.5)).then_inc(capped_ready, 1)
                    if not (isinstance(b, int) and b == 0 and u == 0 and s < 2):
                        act.wait_ge(attend_done, step_index(b, u, s) - 1)
                    for g in range(len(groups)):
                        n = group_index(b, u, s, g)
                        act.wait_ge(capped_ready, n + 1)
                        act.activation(probs[:, step_parity(u, s), g, :], capped[:, g, :], ACT.Exp,
                                       scale=SOFTCAP).then_inc(probs_ready, 1)
                elif e[0] == "gelu":
                    half = e[1]
                    act.wait_ge(side_drained, SIDE.before(b, i))
                    for t in range(CT):
                        h = hidden[:, t].rearrange("p f t -> p (f t)")
                        ins = act.activation(h, h, ACT.Gelu)
                    ins.then_inc(gelu_done, 1)

            batches(act, emit)

        @block.tensor
        def _(pe):
            pe.wait_ge(consts, 5)
            pe.wait_ge(w_loaded, 64)
            setup = [0]

            def setup_bank():
                n = setup[0]
                if n >= SIDE_BANKS:
                    pe.wait_ge(setup_drained, n - SIDE_BANKS + 1)
                setup[0] += 1
                return side[n % SIDE_BANKS]

            for w in range(4):
                bank = setup_bank()
                for kt in range(KT):
                    for o in range(KT):
                        ins = pe.transpose(bank[:, (kt * KT + o) * P:(kt * KT + o + 1) * P],
                                           w_in[:, w, o, kt * P:(kt + 1) * P], ident[:, :])
                ins.then_inc(setup_filled, 1)
            for w in range(2):
                pe.wait_ge(ternary, w + 1)
                bank = setup_bank()
                pe.matmul(bank[:, 0:1], ones[:, :], tern[:, w, 0:1], start=True, stop=True).then_inc(setup_filled, 1)
            bank = setup_bank()
            pe.wait_ge(bias_loaded, 32)
            pe.matmul(bank[:, 0:DIM], ones[0:1, :], b2_row[0:1, :], start=True, stop=True).then_inc(setup_filled, 1)
            pe.wait_ge(ternary, 3)
            for kt in range(KT):
                bank = setup_bank()
                for f in range(FT):
                    ins = pe.transpose(bank[:, :].bitcast(FP16)[:, f * P:(f + 1) * P],
                                       w1_tern[:, f, kt * P:(kt + 1) * P], ident16[:, :])
                ins.then_inc(setup_filled, 1)
            pe.wait_ge(ternary, 4)
            for f2 in range(FT // 2):
                bank = setup_bank()
                for k in range(4):
                    f, o = 2 * f2 + k // 2, k % 2
                    ins = pe.transpose(bank[:, k * P:(k + 1) * P], w2_tern[:, o, f * P:(f + 1) * P], ident[:, :])
                ins.then_inc(setup_filled, 1)
            pe.wait_ge(setup_drained, SETUP_BANKS)

            def scores_step(b, u, s):
                par = u % 2
                groups, _ = STEPS[unit_half(u)][s]
                n0 = group_index(b, u, s, 0)
                for g, pieces in enumerate(groups):
                    prev = last_in_buffer(b, u, s, g)
                    if prev is not None:
                        pe.wait_ge(capped_ready, prev)
                    for h, kt, off, width, q0 in pieces:
                        r = 64 * (h % 2)
                        ins = pe.matmul(scores[:, g, off:off + width],
                                        kT[r:r + 64, par, kt // CT, h // 2, (kt % CT) * P:(kt % CT + 1) * P],
                                        qT[r:r + 64, par, h // 2, q0:q0 + width], start=True, stop=True)
                    ins.then_inc(scores_ready, 1)
                return n0

            def attend_step(b, u, s):
                half, par = unit_half(u), u % 2
                groups, diag = STEPS[half][s]
                if s == 0:
                    pe.wait_ge(v_staged, b * UNITS + u + 1)
                    if not (isinstance(b, int) and b == 0 and u == 0):
                        pe.wait_ge(yT_copied, b * UNITS + u)
                if diag:
                    in_unit = sum(len(x) for x, m in STEPS[half][:s + 1] if m)
                    pe.wait_ge(masked, b * BATCH_MASKS + before_unit(UNIT_MASKS, u) + in_unit)
                else:
                    pe.wait_ge(probs_ready, group_index(b, u, s, len(groups) - 1) + 1)
                pieces = [(g, x) for g, xs in enumerate(groups) for x in xs]
                pieces.sort(key=lambda gx: (gx[1][1], gx[1][0]))
                for g, (h, kt, off, width, q0) in pieces:
                    ins = pe.matmul(attended[32 * h:32 * h + 32, q0:q0 + width], v_unit[:, par, kt, h, :],
                                    probs[:, step_parity(u, s), g, off:off + width], start=(s == 0),
                                    stop=(s == UNIT_STEPS[half] - 1), skip_group_check=True)
                ins.then_inc(attend_done, 1)

            def side_bank(b, local, in_prologue, own_wait):
                base = 0 if in_prologue else SIDE.batch(b)
                (hold if own_wait else lambda e, *x: e.wait_ge(*x))(pe, side_drained, base + max(local - SIDE_BANKS + 1, 0))
                return side[local % SIDE_BANKS]

            def emit(b, i, e, events=None, local=None):
                kind = e[0]
                if local is None:
                    local = counted(PLANS[kind_of(b)][:i], SIDE.weigh)
                if kind == "scores":
                    _, u, s = e
                    if s == 0:
                        pe.wait_ge(side_drained, prep_done(b, i, u))
                    scores_step(b, u, s)
                elif kind == "attend":
                    attend_step(b, e[1], e[2])
                if kind not in SIDE_JOBS:
                    return
                if kind == "fin":
                    pe.wait_ge(yT_copied, (b + e[2]) * UNITS + e[1] + 1)
                elif kind in ("prep_q", "prep_k"):
                    u = e[1]
                    bb = b + u // UNITS
                    need = parts_needed(unit_half(u))
                    pe.wait_ge(parts_ready, (b + u // UNITS) * PAIRS + need)
                elif kind == "xt":
                    pair, ahead = e[1], e[2]
                    pe.wait_ge(x_loaded[pair % 2], ((b + ahead) * (PAIRS // 2) + pair // 2 + 1) * 16)
                elif kind in ("qk", "v", "wo", "f1", "x1t"):
                    if kind == "x1t":
                        pe.wait_ge(x1_ready, WOS.before(b, i))
                    elif kind in ("qk", "v"):
                        pass
                bank = side_bank(b, local, events is not None, kind in ("prep_q", "prep_k"))
                bank16 = bank[:, :].bitcast(FP16)
                if kind == "fin":
                    for t in range(CT):
                        ins = pe.transpose(bank[:, t * P:(t + 1) * P], yT_unit[:, t * P:(t + 1) * P], ident[:, :])
                elif kind in ("prep_q", "prep_k"):
                    is_k = kind == "prep_k"
                    first = CT * e[2] if is_k else CT * unit_half(u)
                    for hp in range(2):
                        for t in range(CT):
                            h0 = GROUP_HEADS * (u % HGS) + 2 * hp
                            src = qk_parts[:, int(is_k), kept_at(bb, first + t, 1), h0:h0 + 2, :]\
                                .rearrange("p a h c -> p (a h c)")
                            ins = pe.transpose(bank16[:, hp * CHUNK + t * P:hp * CHUNK + (t + 1) * P],
                                               src, ident16[:, :])
                elif kind == "xt":
                    t = e[3]
                    for kt in range(KT):
                        ins = pe.transpose(bank[:, kt * P:(kt + 1) * P],
                                           x_in[:, e[1] % 2, t, kt * P:(kt + 1) * P], ident[:, :])
                elif kind in ("qk", "v"):
                    t = e[3]
                    pe.wait_ge(side_drained, xt_done(b, i, e, events))
                    c0, c1 = (0, 2 * DIM) if kind == "qk" else (2 * DIM, 3 * DIM)
                    for kt in range(KT):
                        ins = pe.matmul(bank[:, 0:c1 - c0], xT[:, t, kt, :], w_qkvT[:, kt, c0:c1],
                                        start=(kt == 0), stop=(kt == KT - 1))
                elif kind == "yt":
                    _, half, t, back = e
                    pe.wait_ge(side_drained, last_before(b, i, "fin"))
                    for kt in range(KT):
                        ins = pe.transpose(bank[:, kt * P:(kt + 1) * P],
                                           y_tok[:, half, t, kt * P:(kt + 1) * P], ident[:, :])
                elif kind == "wo":
                    pe.wait_ge(side_drained, last_before(b, i, "yt"))
                    for kt in range(KT):
                        ins = pe.matmul(bank[:, 0:DIM], yT[:, kt, :], w_oT[:, kt, :], start=(kt == 0),
                                        stop=(kt == KT - 1))
                elif kind == "x1t":
                    for part in range(2):
                        for kt in range(KT):
                            c = (part * KT + kt) * P
                            ins = pe.transpose(bank16[:, c:c + P], x1_parts[:, part, kt * P:(kt + 1) * P],
                                               ident16[:, :])
                elif kind == "f1":
                    pe.wait_ge(side_drained, last_before(b, i, "x1t"))
                    for f in range(FT // 2):
                        ft = FT // 2 * e[4] + f
                        for k in range(2 * KT):
                            ins = pe.matmul(bank[:, f * P:(f + 1) * P], w1T[:, k % KT, ft * P:(ft + 1) * P],
                                            x1T[:, k // KT, k % KT, :], start=(k == 0), stop=(k == 2 * KT - 1))
                elif kind == "f2":
                    _, half, t, back = e
                    pe.wait_ge(gelu_done, GELUS.before(b, i))
                    for ft in range(FT):
                        ins = pe.matmul(bank[:, 0:DIM], hidden[:, t, ft, :], w2T[:, ft, :],
                                        start=(ft == 0), stop=(ft == FT - 1))
                ins.then_inc(side_filled, 1)

            def last_before(b, i, name):
                events = PLANS[kind_of(b)]
                return SIDE.before(b, max(k for k in range(i) if events[k][0] == name) + 1)

            def prep_done(b, i, u):
                events = PLANS[kind_of(b)]
                return SIDE.before(b, max(k for k in range(i) if events[k][0] in ("prep_q", "prep_k")) + 1)

            def xt_done(b, i, e, events):
                if events is not None:
                    return counted(events[:max(k for k in range(i) if events[k][0] == "xt") + 1], SIDE.weigh)
                return last_before(b, i, "xt")

            for i, e in enumerate(PROLOGUE):
                local = counted(PROLOGUE[:i], SIDE.weigh)
                if e[0] == "scores":
                    pe.wait_ge(side_drained, local)
                    scores_step(0, 0, 0)
                else:
                    emit_prologue(pe, e, i, local, emit)
            batches(pe, emit)

        @block.vector
        def _(dve):
            links = [0]

            def link(ins, wait=dve.wait_ge):
                links[0] += 1
                ins.then_inc(linked, 1)
                wait(linked, link_base[0] + links[0])

            link_base = [0]
            drained = [0]

            def drain_setup(out_ap, in_fn):
                n = drained[0]
                drained[0] += 1
                dve.wait_ge(setup_filled, n + 1)
                dve.tensor_copy(out_ap, in_fn(side[n % SIDE_BANKS])).then_inc(setup_drained, 1)

            for w in range(4):
                dst = w_oT[:, :, :] if w == 3 else w_qkvT[:, :, w * DIM:(w + 1) * DIM]
                drain_setup(dst, lambda s: s[:, :].rearrange("p (k c) -> p k c", k=KT))
            for w, (src, arrived) in enumerate(((w1_in, w1_loaded), (w2_in, w2_loaded))):
                dve.wait_ge(arrived, 16)
                dve.tensor_reduce(tern[:, w, 0:1], src[:, :, :].rearrange("p a c -> p (a c)"), AX.X, ALU.add,
                                  apply_absolute_value=True).then_inc(ternary, 1)
            for w in range(2):
                n = drained[0]
                drained[0] += 1
                dve.wait_ge(setup_filled, n + 1)
                link(dve.tensor_scalar(tern[:, w, 1:2], side[n % SIDE_BANKS][:, 0:1], 1.0 / (FF * DIM), 1e-8,
                                       ALU.mult, ALU.max))
                link(dve.tensor_scalar(tern[:, w, 2:3], tern[:, w, 1:2], 0.5, None, ALU.mult))
                dve.tensor_scalar(tern[:, w, 3:4], tern[:, w, 1:2], -0.5, None, ALU.mult).then_inc(setup_drained, 1)
                dve.wait_ge(setup_drained, n + 1)
            drain_setup(b2_all[:, :], lambda s: s[:, 0:DIM])
            for w, (src, dst) in enumerate(((w1_in, w1_tern), (w2_in, w2_tern))):
                flat = src[:, :, :].rearrange("p a c -> p (a c)")
                link(dve.tensor_scalar(w_neg[:, :], flat, tern[:, w, 3:4], None, ALU.is_lt))
                dve.scalar_tensor_tensor(dst[:, :, :].rearrange("p a c -> p (a c)"), flat, tern[:, w, 2:3],
                                         w_neg[:, :], op0=ALU.is_gt, op1=ALU.subtract).then_inc(ternary, 1)
                dve.wait_ge(ternary, 3 + w)
            for kt in range(KT):
                drain_setup(w1T[:, kt, :], lambda s: s[:, :].bitcast(FP16))
            for f2 in range(FT // 2):
                drain_setup(w2T[:, 2 * f2:2 * f2 + 2, :].rearrange("p f c -> p (f c)"), lambda s: s[:, :])
            assert drained[0] == SETUP_BANKS and links[0] == SETUP_LINKS

            def normalise(b, pair, ahead):
                flat = qk_raw[:, :, :].rearrange("p t c -> p (t c)")
                n = PAIRS * (b + ahead) + pair
                if not (isinstance(n, int) and n == 0):
                    dve.wait_ge(parts_ready, n)
                link(dve.tensor_tensor(qk_norm[:, :, :].rearrange("p t c -> p (t c)"), flat, flat, ALU.mult))
                link(dve.tensor_reduce(ssq[:, :], qk_norm[:, :, :].rearrange("p t (h d) -> p (t h) d", d=HEAD_DIM),
                                       AX.X, ALU.add))
                link(dve.tensor_scalar(ssq[:, :], ssq[:, :], 1.0 / HEAD_DIM, RMS_EPS, ALU.mult, ALU.add))
                link(dve.tensor_scalar(rms[:, 0, :].bitcast(INT32), ssq[:, :].bitcast(INT32), -0.5, float(0x5F3759DF),
                                       ALU.mult, ALU.add))
                for k in range(3):
                    y, y2 = rms[:, k % 2, :], rms[:, (k + 1) % 2, :]
                    link(dve.tensor_tensor(newton[:, :], y, y, ALU.mult))
                    link(dve.scalar_tensor_tensor(newton[:, :], newton[:, :], -0.5, ssq[:, :], op0=ALU.mult,
                                                  op1=ALU.mult))
                    link(dve.scalar_tensor_tensor(y2, newton[:, :], 1.5, y, op0=ALU.add, op1=ALU.mult))
                link(dve.tensor_tensor(qk_norm[:, :, :].rearrange("p t (h d) -> p (t h) d", d=HEAD_DIM),
                                       qk_raw[:, :, :].rearrange("p t (h d) -> p (t h) d", d=HEAD_DIM),
                                       rms[:, 1, :].unsqueeze(2).to_broadcast([P, 64, HEAD_DIM]), ALU.mult))
                for t in range(2):
                    for which in range(2):
                        high, _ = part_slots(b + ahead, 2 * pair + t, which)
                        ins = dve.tensor_copy(high, head_view(t, which))
                ins.then_inc(high_ready, 1)

            def layernorm(b, i, src, dst):
                link(dve.bn_stats(stats[:, :], src), wait=lambda *x: hold(dve, *x))
                link(dve.bn_aggr(mean_var[:, :], stats[:, :]))
                dve.tensor_scalar(var_eps[:, :], mean_var[:, 1:2], LN_EPS, None, ALU.add).then_inc(var_ready, 1)
                dve.wait_ge(inv_std_ready, LN.before(b, i) + 1)
                return dve.tensor_scalar(dst, src, mean_var[:, 0:1], inv_std[:, 0:1], ALU.subtract, ALU.mult)

            def emit(b, i, e, n=None, local=None, base=None):
                kind = e[0]
                if base is None:
                    base = LINK.before(b, i)
                link_base[0], links[0] = base, 0
                if kind == "norm":
                    normalise(b, e[1], e[2])
                    assert links[0] == LINKS["norm"], links[0]
                if kind not in SIDE_JOBS:
                    return
                if n is None:
                    n = SIDE.before(b, i)
                    local = counted(PLANS[kind_of(b)][:i], SIDE.weigh)
                bank = side[local % SIDE_BANKS]
                bank16 = bank[:, :].bitcast(FP16)
                if kind == "fin":
                    _, u, back = e
                    bb = b + back
                    dve.wait_ge(attend_done, step_index(bb, u, 0) + UNIT_STEPS[unit_half(u)])
                    dve.tensor_copy(yT_unit[:, :], attended[:, :]).then_inc(yT_copied, 1)
                dve.wait_ge(side_filled, n + 1)
                if kind == "fin":
                    hg = u % HGS
                    view = bank[:, :].rearrange("p (t h d) -> p t h d", t=CT, h=GROUP_HEADS)
                    link(dve.reciprocal(inv_den[:, :].rearrange("p (t h) -> p t h", t=CT), view[:, :, :, HEAD_DIM]))
                    dst = y_tok[:, unit_half(u)].rearrange("p t (h d) -> p t h d", d=HEAD_DIM)
                    dve.tensor_tensor(dst[:, :, GROUP_HEADS * hg:GROUP_HEADS * (hg + 1), :],
                                      view[:, :, :, 0:HEAD_DIM],
                                      inv_den[:, :].rearrange("p (t h) -> p t h", t=CT).unsqueeze(3)
                                      .to_broadcast([P, CT, GROUP_HEADS, HEAD_DIM]), ALU.mult)\
                        .then_inc(side_drained, 1)
                elif kind == "prep_q":
                    dve.tensor_copy(qT[:, e[1] % 2].rearrange("p h c -> p (h c)"), bank16).then_inc(side_drained, 1)
                elif kind == "prep_k":
                    dve.tensor_copy(kT[:, e[1] % 2, e[2]].rearrange("p h c -> p (h c)"), bank16)\
                        .then_inc(side_drained, 1)
                elif kind == "xt":
                    dve.tensor_copy(xT[:, e[3]].rearrange("p k c -> p (k c)"), bank[:, 0:DIM])\
                        .then_inc(side_drained, 1)
                elif kind == "qk":
                    dve.tensor_copy(qk_raw[:, e[3], :], bank[:, :]).then_inc(side_drained, 1)
                    dve.wait_ge(side_drained, n + 1)
                elif kind == "v":
                    dve.tensor_copy(values[:, kept_at(b + e[2], 2 * e[1] + e[3], 1), :]
                                    .rearrange("p a c -> p (a c)"), bank[:, 0:DIM]).then_inc(side_drained, 1)
                elif kind == "yt":
                    dve.tensor_copy(yT[:, :, :].rearrange("p k c -> p (k c)"), bank[:, 0:DIM])\
                        .then_inc(side_drained, 1)
                elif kind == "wo":
                    _, half, t, back = e
                    bb = b + back
                    dve.wait_ge(res_loaded[t % 2], (bb * (TILES // 2) + (CT * half + t) // 2 + 1) * 16)
                    dve.tensor_tensor(z[:, 0, :], bank[:, 0:DIM], x_res[:, t % 2, :], ALU.add)\
                        .then_inc(side_drained, 1)
                    dve.wait_ge(side_drained, n + 1)
                    w = WOS.before(b, i)
                    if not (isinstance(w, int) and w == 0):
                        dve.wait_ge(x1_b2_ready, w)
                    link(layernorm(b, i, z[:, 0, :], x1[:, :]))
                    link(dve.tensor_copy(x1_parts[:, 0, :], x1[:, :]))
                    dve.tensor_tensor(x1_parts[:, 1, :], x1[:, :], x1_parts[:, 0, :], ALU.subtract)\
                        .then_inc(x1_ready, 1)
                elif kind == "x1t":
                    dve.tensor_copy(x1T[:, :, :, :].rearrange("p a k c -> p (a k c)"), bank16[:, 0:2 * DIM])\
                        .then_inc(side_drained, 1)
                elif kind == "f1":
                    _, half, t, back, a = e
                    fs = slice(FT // 2 * a, FT // 2 * (a + 1))
                    dve.tensor_tensor(hidden[:, t, fs, :], bank[:, :].rearrange("p (f t) -> p f t", t=P),
                                      b1_col[:, fs].unsqueeze(2).to_broadcast([P, FT // 2, P]), ALU.add)\
                        .then_inc(side_drained, 1)
                elif kind == "f2":
                    _, half, t, back = e
                    dve.tensor_tensor(z[:, 1 + t % 2, :], bank[:, 0:DIM], x1_b2[:, half, t, :], ALU.add)\
                        .then_inc(side_drained, 1)
                    dve.wait_ge(side_drained, n + 1)
                    dve.wait_ge(y_out_free[t % 2], stored_before(b, i, t) + 16)
                    layernorm(b, i, z[:, 1 + t % 2, :], y_out[:, t % 2, :]).then_inc(out_ready, 1)
                assert links[0] == LINKS.get(kind, 0), (kind, links[0])

            def stored_before(b, i, t):
                c = Count(lambda e: 16 * int(e[0] == "f2" and e[2] % 2 == t % 2))
                return c.before(b, i)

            dve.wait_ge(bias_loaded, 32)
            base = SETUP_LINKS
            for i, e in enumerate(PROLOGUE):
                n = counted(PROLOGUE[:i], SIDE.weigh)
                emit(0, None, e, n=n, local=n, base=base)
                base += LINKS.get(e[0], 0)
            batches(dve, emit)


SETUP_BANKS = 4 + 2 + 1 + KT + FT // 2
SETUP_LINKS = 4 + 2
LINK.prologue += SETUP_LINKS


def parts_needed(half):
    return PAIRS if half else PAIRS // 2


def emit_prologue(pe, e, i, local, emit):
    if e[0] != "norm":
        emit(0, i, e, events=PROLOGUE, local=local)


_INS = ["L0_attn_x", "L0_attn_w_q", "L0_attn_w_k", "L0_attn_w_v", "L0_attn_w_o",
        "L0_ffn_W1", "L0_ffn_b1", "L0_ffn_W2", "L0_ffn_b2"]


def kernel(**inputs):
    import numpy as np
    import concourse.bacc as bacc
    from concourse.bass_utils import run_bass_kernel_spmd

    nc = bacc.Bacc("TRN2", target_bir_lowering=False, num_devices=1)
    arrays, args = {}, []
    for name in _INS:
        a = np.ascontiguousarray(inputs[name])
        arrays[f"in_{name}"] = a
        args.append(nc.dram_tensor(f"in_{name}", a.shape, mybir.dt.from_np(a.dtype), kind="ExternalInput").ap())
    args.append(nc.dram_tensor("out", (BATCH, SEQ, DIM), FP32, kind="ExternalOutput").ap())
    build(nc, *args)
    r = run_bass_kernel_spmd(nc, [arrays], core_ids=[0])
    return r.results[0]["out"]
```

```python
from contextlib import ExitStack

import concourse.bass as bass
from concourse import mybir

FP32, FP16, INT32 = mybir.dt.float32, mybir.dt.float16, mybir.dt.int32
ACT = mybir.ActivationFunctionType
ALU = mybir.AluOpType
AX = mybir.AxisListType

BATCH, SEQ, DIM = 4, 1024, 256
HEADS, HEAD_DIM, FF = 16, 16, 1024
SOFTCAP = 50.0
RMS_EPS, LN_EPS = 1.1920929e-07, 1e-05
P = 128
TILES = SEQ // P
CHUNK = 512
CT = CHUNK // P
GROUP_HEADS = 4
HGS = HEADS // GROUP_HEADS
UNITS = 2 * HGS
KT = DIM // P
FT = FF // P
GROUP = 1024
SIDE_BANKS = 3

def steps_of(half):
    steps = []
    for kt in range(CT * half):
        steps.append(([[(h, kt, (h % 2) * 512, 512, 0) for h in (2 * g, 2 * g + 1)] for g in range(2)], None))
    d = CT * half
    steps.append(([[(h, d, (h % 2) * 512, 512, 0) for h in (2 * g, 2 * g + 1)] for g in range(2)],
                  (2, 512, 1, 0)))
    steps.append(([[x for h in (2 * g, 2 * g + 1) for x in ((h, d + 1, (h % 2) * 512, 384, 128),
                                                           (h, d + 3, (h % 2) * 512 + 384, 128, 384))]
                   for g in range(2)], (2, 512, 2, 384)))
    steps.append(([[(h, d + 2, (h % 2) * 512 + (h // 2) * 256, 256, 256) for h in range(4)]], (4, 256, 1, 0)))
    return steps


STEPS = [steps_of(0), steps_of(1)]
UNIT_STEPS = [len(s) for s in STEPS]
UNIT_GROUPS = [sum(len(g) for g, _ in s) for s in STEPS]
UNIT_MASKS = [sum(len(g) for g, m in s if m) for s in STEPS]


def before_unit(per_half, u):
    return sum(per_half[v // HGS] if v < UNITS else 0 for v in range(u)) if u < UNITS else HGS * sum(per_half)


BATCH_STEPS, BATCH_GROUPS, BATCH_MASKS = (HGS * sum(x) for x in (UNIT_STEPS, UNIT_GROUPS, UNIT_MASKS))

SIDE_JOBS = ("w_qkv", "w_o", "b2", "h_scale", "t_mean", "w1", "w2",
             "fin", "prep_q", "prep_k", "xt", "qk", "v", "yt", "wo", "x1t", "f1", "f2")


def plan(kind):
    out = []
    if kind == "end":
        out += [("mask", UNITS - 1, UNIT_STEPS[1] - 1, -1), ("attend", UNITS - 1, UNIT_STEPS[1] - 1, -1),
                ("copy", UNITS - 1, -1), ("gelu", 0, -1), ("split", 0, 0, -1), ("fin", UNITS - 1, -1)]
        for t in range(CT + 2):
            if t < CT:
                out.append(("yt", 1, t, -1))
            if 0 < t <= CT:
                out.append(("wo", 1, t - 1, -1))
                out.append(("ln1", 1, t - 1, -1))
            if t < CT:
                out.append(("f2", 0, t, -1))
                if t + 1 < CT:
                    out.append(("split", 0, t + 1, -1))
                out.append(("ln2", 0, t, -1))
            if 0 < t <= CT:
                out.append(("add_b2", 1, t - 1, -1))
            if t > 1:
                out += [("x1t", 1, t - 2, -1), ("f1", 1, t - 2, -1, 0), ("f1", 1, t - 2, -1, 1)]
        out.append(("gelu", 1, -1))
        for t in range(CT):
            out.append(("split", 1, t, -1))
            if t:
                out.append(("ln2", 1, t - 1, -1))
            out.append(("f2", 1, t, -1))
        return out + [("ln2", 1, CT - 1, -1)]
    for u in range(UNITS):
        half, hg = divmod(u, HGS)
        n = UNIT_STEPS[half]
        slots = {(s, w): [] for s in range(n) for w in (0, 1)}
        post1 = None if kind == "first" and half == 0 else (1 - half, hg, -1 if half == 0 else 0)
        post2 = None if kind == "first" else (half, hg, -1)
        if hg == 0 and post2:
            out.append(("gelu", half, -1))
        before = (u - 1, UNIT_STEPS[(u - 1) // HGS] - 1, 0) if u else (UNITS - 1, UNIT_STEPS[1] - 1, -1)
        if kind == "first" and u == 0:
            before = None
        if before:
            slots[0, 1].append(("copy", before[0], before[2]))
            slots[1, 0].append(("fin", before[0], before[2]))
        nxt = [] if kind == "last" and u == UNITS - 1 else [("prep_q", u + 1), ("prep_k", u + 1, 0)]
        if nxt and HGS <= u + 1 < UNITS:
            nxt.append(("prep_k", u + 1, 1))
        pair = None
        if half == 1 and kind != "last":
            pair = (hg, 1)
        if half == 0 and kind == "first" and hg < 2:
            pair = (2 + hg, 0)
        if half == 0:
            slots[0, 0] += nxt[:1]
            if pair:
                slots[0, 0] += [("xt", *pair, 0), ("xt", *pair, 1)]
                slots[0, 1] += [("qk", *pair, 0), ("v", *pair, 0)]
            if post1:
                slots[1, 0].append(("yt", *post1))
            if post2:
                slots[1, 0].append(("split", *post2))
            slots[1, 0] += nxt[1:]
            if post1:
                slots[1, 1] += [("wo", *post1)]
                slots[2, 0].append(("ln1", *post1))
            if pair:
                slots[1, 1] += [("qk", *pair, 1), ("v", *pair, 1), ("norm0", *pair), ("norm1", *pair),
                                ("norm2", *pair), ("low", *pair)]
            if nxt:
                slots[1, 1].append(("stage", u + 1))
            if post2:
                slots[2, 0].append(("f2", *post2))
            if post1:
                slots[2, 0].append(("x1t", *post1))
                slots[2, 1] += [("f1", *post1, 0), ("add_b2", *post1), ("f1", *post1, 1)]
            if post2:
                slots[2, 1] += [("ln2", *post2)]
            if kind == "first":
                slots[2, 1] += [[("w_o",), ("b2",)],
                                [("h_sum",), ("h_scale",), ("t_sum", 0), ("t_mean", 0), ("t_sum", 1), ("t_mean", 1)],
                                [("t_make", 0), ("w1", 0), ("w1", 1)],
                                [("t_make", 1), ("w2", 0), ("w2", 1)]][hg]
        else:
            if pair:
                slots[0, 0] += [("xt", *pair, 0), ("xt", *pair, 1)]
                slots[0, 1] += [("qk", *pair, 0), ("v", *pair, 0)]
                slots[1, 0] += [("qk", *pair, 1), ("v", *pair, 1)]
                slots[1, 1] += [("norm0", *pair)]
                slots[2, 0] += [("norm1", *pair)]
                slots[3, 0] += [("norm2", *pair), ("low", *pair)]
            slots[2, 0].insert(0, ("yt", *post1))
            slots[3, 0].append(("wo", *post1))
            if post2:
                slots[2, 1].append(("split", *post2))
                slots[3, 1].append(("f2", *post2))
            slots[3, 1].append(("ln1", *post1))
            if post2:
                slots[4, 0].append(("ln2", *post2))
            slots[4, 0] += nxt[:1]
            slots[4, 1] += [("add_b2", *post1), ("x1t", *post1)]
            slots[5, 0] += nxt[1:]
            slots[5, 1] += [("f1", *post1, 0)]
            slots[6, 0] += [("f1", *post1, 1)]
            if nxt:
                slots[1, 1].append(("stage", u + 1))
        for s in range(n):
            out.append(("softmax", u, s))
            if s + 1 < n:
                out.append(("scores", u, s + 1))
            elif not (kind == "last" and u == UNITS - 1):
                out.append(("scores", u + 1, 0))
            prev = (u, s - 1, 0) if s else before
            if prev:
                out.append(("mask", *prev))
            out += slots[s, 0]
            if prev:
                out.append(("attend", *prev))
            out += slots[s, 1]
    return out


PLANS = {k: plan(k) for k in ("first", "middle", "last", "end")}
PROLOGUE = ([("w_qkv", w) for w in range(3)]
            + [x for p in (0, 1) for x in (("xt", p, 0, 0), ("xt", p, 0, 1), ("qk", p, 0, 0), ("v", p, 0, 0),
                                           ("qk", p, 0, 1), ("v", p, 0, 1), ("norm0", p, 0), ("norm1", p, 0),
                                           ("norm2", p, 0), ("low", p, 0))]
            + [("prep_q", 0), ("prep_k", 0, 0), ("scores", 0, 0)])
LINKS = {"fin": 1, "norm0": 2, "norm1": 8, "norm2": 4, "wo": 2, "ln1": 2, "f2": 2, "split": 1, "h_scale": 4, "t_mean": 1, "t_make": 1}
PAIRS = TILES // 2


def kind_of(b):
    return {0: "first", BATCH - 1: "last", BATCH: "end"}.get(b, "middle") if isinstance(b, int) else "middle"


def counted(events, weigh):
    return sum(weigh(e) for e in events)


class Count:

    def __init__(self, weigh):
        self.weigh = weigh
        self.prologue = counted(PROLOGUE, weigh)
        self.first = counted(PLANS["first"], weigh)
        self.middle = counted(PLANS["middle"], weigh)
        self.last = counted(PLANS["last"], weigh)

    def batch(self, b):
        if isinstance(b, int):
            done = [0, self.first]
            for _ in range(1, BATCH - 1):
                done.append(done[-1] + self.middle)
            done.append(done[-1] + self.last)
            return self.prologue + done[b]
        return b * self.middle + (self.prologue + self.first - self.middle)

    def before(self, b, i):
        return self.batch(b) + counted(PLANS[kind_of(b)][:i], self.weigh)


def of(*names):
    return lambda e: int(e[0] in names)


SIDE = Count(of(*SIDE_JOBS))
LINK = Count(lambda e: LINKS.get(e[0], 0))
PAIR = Count(of("low"))
GELUS = Count(of("gelu"))
LN = Count(of("wo", "f2"))
OUTS = Count(of("ln2"))
LN1S = Count(of("ln1"))
ADDS = Count(of("add_b2"))
SPLITS = Count(of("split"))
SUMS = Count(of("h_sum", "t_sum", "t_make"))
COPIES = Count(of("copy"))


def build(nc, x, w_q, w_k, w_v, w_o, W1, b1, W2, b2, out):
    x_t = x.rearrange("b (t p) d -> p (b t) d", p=P)
    out_t = out.rearrange("b (t p) d -> p (b t) d", p=P)
    ctx = ExitStack()
    with ctx:
        def sb(name, shape, dt=FP32):
            return ctx.enter_context(nc.sbuf_tensor(name, shape, dt))

        def sem(name):
            return ctx.enter_context(nc.semaphore(name))

        w_qkvT = sb("w_qkvT", [P, KT, 3 * DIM])
        w_oT = sb("w_oT", [P, KT, DIM])
        w1T = sb("w1T", [P, KT, FF], FP16)
        w2T = sb("w2T", [P, FT, DIM], FP16)
        b1_col = sb("b1_col", [P, FT])
        b2_row = sb("b2_row", [1, DIM])
        b2_all = sb("b2_all", [P, DIM])
        ident = sb("ident", [P, P])
        ident16 = sb("ident16", [P, P], FP16)
        ones = sb("ones", [P, P])
        minus_half = sb("minus_half", [P, 1])
        tern = sb("tern", [P, 2, 4])
        h_scale = sb("h_scale", [P, 6])
        x_in = sb("x_in", [P, 2, 2, DIM])
        xT = sb("xT", [P, 2, KT, P])
        qk_raw = sb("qk_raw", [P, 2, 2 * DIM])
        qk_norm = sb("qk_norm", [P, 2, 2 * DIM])
        ssq = sb("ssq", [P, 64])
        rms = sb("rms", [P, 2, 64])
        newton = sb("newton", [P, 64])
        qk_parts = sb("qk_parts", [P, 2, 2 * TILES, HEADS, 4 * HEAD_DIM], FP16)
        values = sb("values", [P, 2 * TILES, DIM])
        qT = sb("qT", [P, 2, 2, CHUNK], FP16)
        kT = sb("kT", [P, 2, 2, 2, CHUNK], FP16)
        v_unit = sb("v_unit", [P, 2, TILES, GROUP_HEADS, 2 * HEAD_DIM])
        capped = sb("capped", [P, 2, GROUP])
        probs = sb("probs", [P, 2, 2, GROUP])
        yT_unit = sb("yT_unit", [P, CHUNK])
        inv_den = sb("inv_den", [P, CT * GROUP_HEADS])
        y_tok = sb("y_tok", [P, 2, CT, DIM])
        yT = sb("yT", [P, 2, KT, P])
        x_res = sb("x_res", [P, 2, DIM])
        z = sb("z", [P, 3, DIM])
        stats = sb("stats", [P, 6])
        mean_var = sb("mean_var", [P, 2, 2])
        var_eps = sb("var_eps", [P, 2])
        inv_std = sb("inv_std", [P, 2])
        x1 = sb("x1", [P, 2, DIM])
        x1_parts = sb("x1_parts", [P, 2, 2, DIM], FP16)
        x1_b2 = sb("x1_b2", [P, CT, DIM])
        x1T = sb("x1T", [P, 2, 2, KT, P], FP16)
        hidden = sb("hidden", [P, CT, FT, P])
        h_parts = sb("h_parts", [P, 2, FT * P], FP16)
        y_out = sb("y_out", [P, 2, DIM])
        w_in = capped[:, :, :].rearrange("p a (w k d) -> p (a w) k d", k=KT, d=DIM)
        w_o_in = y_out[:, :, :]
        room = hidden[:, :, :, :].rearrange("p t f c -> p (t f c)")
        w1_in = room[:, 0:FF * KT].rearrange("p (f d) -> p f d", d=DIM)
        w2_in = room[:, FF * KT:2 * FF * KT].rearrange("p (o f) -> p o f", f=FF)
        w1_tern = x1_b2[:, :, :].rearrange("p t d -> p (t d)").bitcast(FP16)\
            .rearrange("p (f d) -> p f d", d=DIM)
        w2_tern = h_parts[:, :, :]
        w_neg = qk_norm[:, :, :].rearrange("p t c -> p (t c)").bitcast(FP16)
        h_parts_odd = probs[:, 0, 0, :].bitcast(FP16).rearrange("p (k f) -> p k f", k=2)

        scores = ctx.enter_context(nc.psum_tensor("scores", [P, 2, GROUP], FP32))
        attended = ctx.enter_context(nc.psum_tensor("attended", [P, CHUNK], FP32))
        side = [ctx.enter_context(nc.psum_tensor(f"side{i}", [P, 512], FP32)) for i in range(SIDE_BANKS)]

        w_loaded = sem("w_loaded")
        w_o_loaded = sem("w_o_loaded")
        w1_loaded = sem("w1_loaded")
        w2_loaded = sem("w2_loaded")
        b1_loaded = sem("b1_loaded")
        b2_loaded = sem("b2_loaded")
        x_loaded = [sem("x_loaded0"), sem("x_loaded1")]
        res_loaded = [sem("res_loaded0"), sem("res_loaded1")]
        y_out_free = [sem("y_out_free0"), sem("y_out_free1")]
        consts = sem("consts")
        consts_step = sem("consts_step")
        summed = sem("summed")
        h_split = sem("h_split")
        side_filled = sem("side_filled")
        side_drained = sem("side_drained")
        linked = sem("linked")
        high_ready = sem("high_ready")
        parts_ready = sem("parts_ready")
        v_staged = sem("v_staged")
        scores_ready = sem("scores_ready")
        capped_ready = sem("capped_ready")
        probs_ready = sem("probs_ready")
        masked = sem("masked")
        attend_done = sem("attend_done")
        yT_copied = sem("yT_copied")
        var_ready = sem("var_ready")
        inv_std_ready = sem("inv_std_ready")
        x1_ready = sem("x1_ready")
        x1_b2_ready = sem("x1_b2_ready")
        gelu_done = sem("gelu_done")
        out_ready = sem("out_ready")
        held = [sem(f"held{n}") for n in range(3)]

        block = ctx.enter_context(nc.Block())

        def batches(eng, emit):
            for i, e in enumerate(PLANS["first"]):
                emit(0, i, e)
            with eng.Fori(1, BATCH - 1) as b:
                for i, e in enumerate(PLANS["middle"]):
                    emit(b, i, e)
            for i, e in enumerate(PLANS["last"]):
                emit(BATCH - 1, i, e)
            for i, e in enumerate(PLANS["end"]):
                emit(BATCH, i, e)

        def hold(eng, semaphore, value):
            eng.wait_ge(semaphore, value)
            if not isinstance(value, int):
                eng.sem_inc(held[eng is nc.vector and 0 or eng is nc.tensor and 1 or 2], 1)

        def tiles_at(b, first, n):
            return bass.ds(b * TILES + first, n)

        def kept_at(b, first, n):
            at = (b & 1) * TILES + first
            return slice(at, at + n) if isinstance(at, int) else bass.ds(at, n)

        def part_slots(b, t, which):
            tile = qk_parts[:, which, kept_at(b, t, 1)].rearrange("p a h c -> p (a h) c")
            if which == 0:
                slots = tile.rearrange("p h (r k d) -> p h r k d", r=2, k=2)
                return slots[:, :, :, 0, :], slots[:, :, :, 1, :]
            slots = tile.rearrange("p h (k r d) -> p h k r d", r=2, k=2)
            return slots[:, :, 0, :, :], slots[:, :, 1, :, :]

        def head_view(t, which):
            return qk_norm[:, t, which * DIM:(which + 1) * DIM].rearrange("p (h d) -> p h d", d=HEAD_DIM)\
                .unsqueeze(2).to_broadcast([P, HEADS, 2, HEAD_DIM])

        def group_index(b, u, s, g):
            half = min(u, UNITS - 1) // HGS if u < UNITS else 0
            in_unit = sum(len(x) for x, _ in STEPS[half][:s]) + g
            return b * BATCH_GROUPS + before_unit(UNIT_GROUPS, u) + in_unit

        def step_index(b, u, s):
            return b * BATCH_STEPS + before_unit(UNIT_STEPS, u) + s

        def step_parity(u, s):
            return (before_unit(UNIT_STEPS, u % UNITS) + s) % 2

        def last_in_buffer(b, u, s, g):
            if isinstance(b, int) and b == 0 and u == 0 and s == 0:
                return None
            back, uu, ss = 0, u, s
            while True:
                ss -= 1
                if ss < 0:
                    uu -= 1
                    if uu < 0:
                        uu, back = UNITS - 1, 1
                    ss = UNIT_STEPS[unit_half(uu)] - 1
                if len(STEPS[unit_half(uu)][ss][0]) > g:
                    return group_index(b - back, uu, ss, g) + 1

        def h_parts_of(b, t):
            return h_parts_odd if isinstance(b, int) and b == BATCH and t % 2 else h_parts

        def unit_half(u):
            return (u % UNITS) // HGS

        @block.sync
        def _(sp):
            def load_pair(b, pair):
                sp.dma_start(x_in[:, pair % 2], x_t[:, tiles_at(b, 2 * pair, 2), :]).then_inc(x_loaded[pair % 2], 16)

            def load_residual(b, half, t):
                sp.dma_start(x_res[:, t % 2], x_t[:, b * TILES + CT * half + t, :] if isinstance(b, int)
                             else x_t[:, bass.ds(b * TILES + CT * half + t, 1), :].rearrange("p a d -> p (a d)"))\
                    .then_inc(res_loaded[t % 2], 16)

            load_pair(0, 0)
            load_pair(0, 1)
            load_residual(0, 0, 0)
            load_residual(0, 0, 1)
            for p in (0, 1):
                sp.wait_ge(side_drained, 3 + 2 + 6 * p)
                load_pair(0, p + 2)

            def emit(b, i, e):
                if e[0] == "xt" and e[3] == 1:
                    pair, ahead = e[1], e[2]
                    if ahead == 0 or pair + 2 < PAIRS:
                        sp.wait_ge(side_drained, SIDE.before(b, i) + 1)
                        load_pair(b + 1, pair - 2 if ahead == 0 else pair + 2)
                if i == 0 and kind_of(b) == "middle":
                    sp.wait_ge(side_drained, SIDE.batch(b))
                    load_pair(b + 1, 0)
                    load_pair(b + 1, 1)
                if e[0] == "wo":
                    _, half, t, back = e
                    sp.wait_ge(side_drained, SIDE.before(b, i) + 1)
                    nb = b + back
                    if t + 2 < CT:
                        load_residual(nb, half, t + 2)
                    elif half == 0:
                        load_residual(nb, 1, t - 2)
                    elif not (isinstance(b, int) and b == BATCH):
                        load_residual(nb + 1, 0, t - 2)
                if e[0] == "ln2":
                    _, half, t, back = e
                    sp.wait_ge(out_ready, OUTS.before(b, i) + 1)
                    nb = b + back
                    dst = out_t[:, bass.ds(nb * TILES + CT * half + t, 1), :].rearrange("p a d -> p (a d)") \
                        if not isinstance(nb, int) else out_t[:, nb * TILES + CT * half + t, :]
                    sp.dma_start(dst, y_out[:, t % 2]).then_inc(y_out_free[t % 2], 16)

            for par in range(2):
                sp.sem_inc(y_out_free[par], 16)
            batches(sp, emit)
            for par in range(2):
                sp.wait_ge(y_out_free[par], 16 + 16 * BATCH * TILES // 2)

        @block.gpsimd
        def _(pool):
            pool.memset(ident[:, :], 0.0).then_inc(consts_step, 1)
            pool.memset(ident16[:, :], 0.0).then_inc(consts_step, 1)
            pool.wait_ge(consts_step, 2)
            for m in (ident, ident16):
                pool.affine_select(out=m[:, :], in_=m[:, :], compare_op=ALU.not_equal, fill=1.0, base=0,
                                   pattern=[[-1, P]], channel_multiplier=1).then_inc(consts, 1)
            pool.memset(ones[:, :], 1.0).then_inc(consts, 1)
            pool.memset(minus_half[:, :], -0.5).then_inc(consts, 1)
            pool.memset(v_unit[:, :, :, :, HEAD_DIM:], 1.0).then_inc(consts, 1)
            pool.wait_ge(consts, 5)

            def low_parts(b, i, pair, ahead, wait):
                pool.wait_ge(high_ready, wait)
                for t in range(2):
                    for which in range(2):
                        high, low = part_slots(b + ahead, 2 * pair + t, which)
                        ins = pool.tensor_tensor(low, head_view(t, which), high, ALU.subtract)
                ins.then_inc(parts_ready, 1)

            def stage_values(b, u):
                n = TILES if unit_half(u) else CT
                hg = u % HGS
                bb = b + u // UNITS
                src = values[:, kept_at(bb, 0, n), GROUP_HEADS * HEAD_DIM * hg:GROUP_HEADS * HEAD_DIM * (hg + 1)]
                pool.tensor_copy(v_unit[:, u % 2, 0:n, :, 0:HEAD_DIM],
                                 src.rearrange("p t (h d) -> p t h d", d=HEAD_DIM)).then_inc(v_staged, 1)

            for p in (0, 1):
                low_parts(0, None, p, 0, p + 1)
            pool.wait_ge(side_drained, 3 + 12)
            stage_values(0, 0)

            def emit(b, i, e):
                if e[0] == "low":
                    low_parts(b, i, e[1], e[2], PAIR.before(b, i) + 1)
                elif e[0] == "stage":
                    u = e[1]
                    pool.wait_ge(side_drained, SIDE.before(b, i))
                    if not (isinstance(b, int) and b == 0 and u < 2):
                        hold(pool, attend_done, step_index(b, u - 1, 0))
                    stage_values(b, u)
                elif e[0] in ("wo", "f2"):
                    pool.wait_ge(var_ready, LN.before(b, i) + 1)
                    k = int(e[0] == "f2")
                    pool.tensor_tensor(inv_std[:, k:k + 1], var_eps[:, k:k + 1], minus_half[:, :], ALU.pow)\
                        .then_inc(inv_std_ready, 1)
                elif e[0] == "add_b2":
                    t = e[2]
                    pool.wait_ge(x1_ready, LN1S.before(b, i))
                    pool.wait_ge(side_drained, SIDE.before(b, i))
                    pool.tensor_tensor(x1_b2[:, t, :], x1[:, t % 2, :], b2_all[:, :], ALU.add)\
                        .then_inc(x1_b2_ready, 1)
                elif e[0] == "mask":
                    _, u, s, back = e
                    groups, diag = STEPS[unit_half(u)][s]
                    if diag:
                        n, stride, m, inner = diag
                        for g in range(len(groups)):
                            hold(pool, probs_ready, group_index(b + back, u, s, g) + 1)
                            buf = probs[:, step_parity(u, s), g, :]
                            for k in range(m):
                                view = buf.rearrange("p (h c) -> p h c", c=stride)[:, :, k * inner:k * inner + P]
                                ins = pool.affine_select(out=view, in_=view, compare_op=ALU.is_ge, fill=0.0,
                                                         base=0, pattern=[[0, n], [1, P]], channel_multiplier=-1)
                            ins.then_inc(masked, 1)

            batches(pool, emit)

        @block.scalar
        def _(act):
            for i, w in enumerate((w_q, w_k, w_v)):
                act.dma_start(w_in[:, i], w.rearrange("(o p) d -> p o d", p=P)).then_inc(w_loaded, 16)
            act.dma_start(w_o_in, w_o.rearrange("(o p) d -> p o d", p=P)).then_inc(w_o_loaded, 16)
            act.dma_start(b2_row[0:1, :], b2.rearrange("(a d) -> a d", a=1)).then_inc(b2_loaded, 16)
            with nc.allow_non_contiguous_dma(reason="1024 biases, once"):
                act.dma_start(b1_col[:, :], b1.rearrange("(f p) -> p f", p=P)).then_inc(b1_loaded, 16)
            act.dma_start(w1_in, W1.rearrange("(f p) d -> p f d", p=P)).then_inc(w1_loaded, 16)
            act.dma_start(w2_in, W2.rearrange("(o p) f -> p o f", p=P)).then_inc(w2_loaded, 16)

            def emit(b, i, e):
                if e[0] == "softmax":
                    _, u, s = e
                    groups, _ = STEPS[unit_half(u)][s]
                    for g in range(len(groups)):
                        n = group_index(b, u, s, g)
                        prev = last_in_buffer(b, u, s, g)
                        if prev is not None:
                            act.wait_ge(probs_ready, prev)
                        act.wait_ge(scores_ready, n + 1)
                        act.activation(capped[:, g, :], scores[:, g, :], ACT.Tanh,
                                       scale=1.0 / (SOFTCAP * HEAD_DIM ** 0.5)).then_inc(capped_ready, 1)
                    if not (isinstance(b, int) and b == 0 and u == 0 and s < 2):
                        act.wait_ge(attend_done, step_index(b, u, s) - 1)
                    for g in range(len(groups)):
                        n = group_index(b, u, s, g)
                        act.wait_ge(capped_ready, n + 1)
                        act.activation(probs[:, step_parity(u, s), g, :], capped[:, g, :], ACT.Exp,
                                       scale=SOFTCAP).then_inc(probs_ready, 1)
                elif e[0] == "gelu":
                    half = e[1]
                    act.wait_ge(side_drained, SIDE.before(b, i))
                    for t in range(CT):
                        h = hidden[:, t].rearrange("p f t -> p (f t)")
                        ins = act.activation(h, h, ACT.Gelu)
                    ins.then_inc(gelu_done, 1)

            batches(act, emit)

        @block.tensor
        def _(pe):
            pe.wait_ge(consts, 5)

            def scores_step(b, u, s):
                par = u % 2
                groups, _ = STEPS[unit_half(u)][s]
                n0 = group_index(b, u, s, 0)
                for g, pieces in enumerate(groups):
                    prev = last_in_buffer(b, u, s, g)
                    if prev is not None:
                        pe.wait_ge(capped_ready, prev)
                    for h, kt, off, width, q0 in pieces:
                        r = 64 * (h % 2)
                        ins = pe.matmul(scores[:, g, off:off + width],
                                        kT[r:r + 64, par, kt // CT, h // 2, (kt % CT) * P:(kt % CT + 1) * P],
                                        qT[r:r + 64, par, h // 2, q0:q0 + width], start=True, stop=True)
                    ins.then_inc(scores_ready, 1)
                return n0

            def attend_step(b, u, s, back):
                half, par = unit_half(u), u % 2
                b = b + back
                groups, diag = STEPS[half][s]
                if s == 0:
                    pe.wait_ge(v_staged, b * UNITS + u + 1)
                    if not (isinstance(b, int) and b == 0 and u == 0):
                        pe.wait_ge(yT_copied, b * UNITS + u)
                if diag:
                    in_unit = sum(len(x) for x, m in STEPS[half][:s + 1] if m)
                    pe.wait_ge(masked, b * BATCH_MASKS + before_unit(UNIT_MASKS, u) + in_unit)
                else:
                    pe.wait_ge(probs_ready, group_index(b, u, s, len(groups) - 1) + 1)
                pieces = [(g, x) for g, xs in enumerate(groups) for x in xs]
                pieces.sort(key=lambda gx: (gx[1][1], gx[1][0]))
                for g, (h, kt, off, width, q0) in pieces:
                    ins = pe.matmul(attended[32 * h:32 * h + 32, q0:q0 + width], v_unit[:, par, kt, h, :],
                                    probs[:, step_parity(u, s), g, off:off + width], start=(s == 0),
                                    stop=(s == UNIT_STEPS[half] - 1), skip_group_check=True)
                ins.then_inc(attend_done, 1)

            def side_bank(b, local, in_prologue, own_wait):
                base = 0 if in_prologue else SIDE.batch(b)
                (hold if own_wait else lambda e, *x: e.wait_ge(*x))(pe, side_drained, base + max(local - SIDE_BANKS + 1, 0))
                return side[local % SIDE_BANKS]

            def emit(b, i, e, events=None, local=None):
                kind = e[0]
                if local is None:
                    local = counted(PLANS[kind_of(b)][:i], SIDE.weigh)
                if kind == "scores":
                    _, u, s = e
                    if s == 0:
                        pe.wait_ge(side_drained, prep_done(b, i, u))
                    scores_step(b, u, s)
                elif kind == "attend":
                    attend_step(b, *e[1:])
                if kind not in SIDE_JOBS:
                    return
                if kind == "fin":
                    pe.wait_ge(yT_copied, (b + e[2]) * UNITS + e[1] + 1)
                elif kind == "w_qkv":
                    pe.wait_ge(w_loaded, 48)
                elif kind == "w_o":
                    pe.wait_ge(w_o_loaded, 16)
                elif kind == "b2":
                    pe.wait_ge(b2_loaded, 16)
                elif kind in ("h_scale", "t_mean", "w1", "w2"):
                    pe.wait_ge(summed, SUMS.before(b, i))
                elif kind in ("prep_q", "prep_k"):
                    u = e[1]
                    bb = b + u // UNITS
                    need = parts_needed(unit_half(u))
                    pe.wait_ge(parts_ready, (b + u // UNITS) * PAIRS + need)
                elif kind == "xt":
                    pair, ahead = e[1], e[2]
                    pe.wait_ge(x_loaded[pair % 2], ((b + ahead) * (PAIRS // 2) + pair // 2 + 1) * 16)
                elif kind in ("qk", "v", "wo", "f1", "x1t"):
                    if kind == "x1t":
                        pe.wait_ge(x1_ready, done(b, i, ("ln1", *e[1:]), LN1S))
                    elif kind in ("qk", "v"):
                        pass
                bank = side_bank(b, local, events is not None, kind in ("prep_q", "prep_k"))
                bank16 = bank[:, :].bitcast(FP16)
                if kind in ("w_qkv", "w_o"):
                    src = w_o_in if kind == "w_o" else w_in[:, e[1]]
                    for kt in range(KT):
                        for o in range(KT):
                            ins = pe.transpose(bank[:, (kt * KT + o) * P:(kt * KT + o + 1) * P],
                                               src[:, o, kt * P:(kt + 1) * P], ident[:, :])
                elif kind == "b2":
                    ins = pe.matmul(bank[:, 0:DIM], ones[0:1, :], b2_row[0:1, :], start=True, stop=True)
                elif kind in ("h_scale", "t_mean"):
                    src = h_scale[:, 0:1] if kind == "h_scale" else tern[:, e[1], 0:1]
                    ins = pe.matmul(bank[:, 0:1], ones[:, :], src, start=True, stop=True)
                elif kind == "w1":
                    for f in range(FT):
                        ins = pe.transpose(bank16[:, f * P:(f + 1) * P],
                                           w1_tern[:, f, e[1] * P:(e[1] + 1) * P], ident16[:, :])
                elif kind == "w2":
                    for k in range(FT):
                        f, o = FT // 2 * e[1] + k // 2, k % 2
                        ins = pe.transpose(bank16[:, k * P:(k + 1) * P], w2_tern[:, o, f * P:(f + 1) * P],
                                           ident16[:, :])
                elif kind == "fin":
                    for t in range(CT):
                        ins = pe.transpose(bank[:, t * P:(t + 1) * P], yT_unit[:, t * P:(t + 1) * P], ident[:, :])
                elif kind in ("prep_q", "prep_k"):
                    is_k = kind == "prep_k"
                    first = CT * e[2] if is_k else CT * unit_half(u)
                    for hp in range(2):
                        for t in range(CT):
                            h0 = GROUP_HEADS * (u % HGS) + 2 * hp
                            src = qk_parts[:, int(is_k), kept_at(bb, first + t, 1), h0:h0 + 2, :]\
                                .rearrange("p a h c -> p (a h c)")
                            ins = pe.transpose(bank16[:, hp * CHUNK + t * P:hp * CHUNK + (t + 1) * P],
                                               src, ident16[:, :])
                elif kind == "xt":
                    t = e[3]
                    for kt in range(KT):
                        ins = pe.transpose(bank[:, kt * P:(kt + 1) * P],
                                           x_in[:, e[1] % 2, t, kt * P:(kt + 1) * P], ident[:, :])
                elif kind in ("qk", "v"):
                    t = e[3]
                    pe.wait_ge(side_drained, xt_done(b, i, e, events))
                    c0, c1 = (0, 2 * DIM) if kind == "qk" else (2 * DIM, 3 * DIM)
                    for kt in range(KT):
                        ins = pe.matmul(bank[:, 0:c1 - c0], xT[:, t, kt, :], w_qkvT[:, kt, c0:c1],
                                        start=(kt == 0), stop=(kt == KT - 1))
                elif kind == "yt":
                    _, half, t, back = e
                    pe.wait_ge(side_drained, last_before(b, i, "fin"))
                    for kt in range(KT):
                        ins = pe.transpose(bank[:, kt * P:(kt + 1) * P],
                                           y_tok[:, half, t, kt * P:(kt + 1) * P], ident[:, :])
                elif kind == "wo":
                    pe.wait_ge(side_drained, done(b, i, ("yt", *e[1:])))
                    for kt in range(KT):
                        ins = pe.matmul(bank[:, 0:DIM], yT[:, e[2] % 2, kt, :], w_oT[:, kt, :], start=(kt == 0),
                                        stop=(kt == KT - 1))
                elif kind == "x1t":
                    for part in range(2):
                        for kt in range(KT):
                            c = (part * KT + kt) * P
                            ins = pe.transpose(bank16[:, c:c + P], x1_parts[:, e[2] % 2, part, kt * P:(kt + 1) * P],
                                               ident16[:, :])
                elif kind == "f1":
                    pe.wait_ge(side_drained, done(b, i, ("x1t", *e[1:4])))
                    for f in range(FT // 2):
                        ft = FT // 2 * e[4] + f
                        for k in range(2 * KT):
                            ins = pe.matmul(bank[:, f * P:(f + 1) * P], w1T[:, k % KT, ft * P:(ft + 1) * P],
                                            x1T[:, e[2] % 2, k // KT, k % KT, :], start=(k == 0), stop=(k == 2 * KT - 1))
                elif kind == "f2":
                    _, half, t, back = e
                    pe.wait_ge(h_split, done(b, i, ("split", *e[1:]), SPLITS))
                    for k in range(2 * FT):
                        part, ft = divmod(k, FT)
                        ins = pe.matmul(bank[:, 0:DIM], h_parts_of(b, t)[:, part, ft * P:(ft + 1) * P],
                                        w2T[:, ft, :], start=(k == 0), stop=(k == 2 * FT - 1))
                ins.then_inc(side_filled, 1)

            def done(b, i, event, count=SIDE):
                k = PLANS[kind_of(b)].index(event)
                assert k < i
                return count.before(b, k + 1)

            def last_before(b, i, name):
                events = PLANS[kind_of(b)]
                return SIDE.before(b, max(k for k in range(i) if events[k][0] == name) + 1)

            def prep_done(b, i, u):
                events = PLANS[kind_of(b)]
                return SIDE.before(b, max(k for k in range(i) if events[k][0] in ("prep_q", "prep_k")) + 1)

            def xt_done(b, i, e, events):
                if events is not None:
                    return counted(events[:max(k for k in range(i) if events[k][0] == "xt") + 1], SIDE.weigh)
                return last_before(b, i, "xt")

            for i, e in enumerate(PROLOGUE):
                local = counted(PROLOGUE[:i], SIDE.weigh)
                if e[0] == "scores":
                    pe.wait_ge(side_drained, local)
                    scores_step(0, 0, 0)
                else:
                    emit_prologue(pe, e, i, local, emit)
            batches(pe, emit)

        @block.vector
        def _(dve):
            links = [0]

            def link(ins, wait=dve.wait_ge):
                links[0] += 1
                ins.then_inc(linked, 1)
                wait(linked, link_base[0] + links[0])

            link_base = [0]
            def squares(b, pair, ahead):
                flat = qk_raw[:, :, :].rearrange("p t c -> p (t c)")
                n = PAIRS * (b + ahead) + pair
                if not (isinstance(n, int) and n == 0):
                    dve.wait_ge(parts_ready, n)
                link(dve.tensor_tensor(qk_norm[:, :, :].rearrange("p t c -> p (t c)"), flat, flat, ALU.mult))
                link(dve.tensor_reduce(ssq[:, :], qk_norm[:, :, :].rearrange("p t (h d) -> p (t h) d", d=HEAD_DIM),
                                       AX.X, ALU.add))

            def inverse_rms():
                link(dve.tensor_scalar(ssq[:, :], ssq[:, :], 1.0 / HEAD_DIM, RMS_EPS, ALU.mult, ALU.add))
                link(dve.tensor_scalar(rms[:, 0, :].bitcast(INT32), ssq[:, :].bitcast(INT32), -0.5, float(0x5F3759DF),
                                       ALU.mult, ALU.add))
                for k in range(2):
                    newton_step(k)

            def newton_step(k):
                y, y2 = rms[:, k % 2, :], rms[:, (k + 1) % 2, :]
                link(dve.tensor_tensor(newton[:, :], y, y, ALU.mult))
                link(dve.scalar_tensor_tensor(newton[:, :], newton[:, :], -0.5, ssq[:, :], op0=ALU.mult,
                                              op1=ALU.mult))
                link(dve.scalar_tensor_tensor(y2, newton[:, :], 1.5, y, op0=ALU.add, op1=ALU.mult))

            def normalise(b, pair, ahead):
                newton_step(2)
                link(dve.tensor_tensor(qk_norm[:, :, :].rearrange("p t (h d) -> p (t h) d", d=HEAD_DIM),
                                       qk_raw[:, :, :].rearrange("p t (h d) -> p (t h) d", d=HEAD_DIM),
                                       rms[:, 1, :].unsqueeze(2).to_broadcast([P, 64, HEAD_DIM]), ALU.mult))
                for t in range(2):
                    for which in range(2):
                        high, _ = part_slots(b + ahead, 2 * pair + t, which)
                        ins = dve.tensor_copy(high, head_view(t, which))
                ins.then_inc(high_ready, 1)

            def statistics(k, src):
                link(dve.bn_stats(stats[:, :], src), wait=lambda *x: hold(dve, *x))
                link(dve.bn_aggr(mean_var[:, k, :], stats[:, :]))
                dve.tensor_scalar(var_eps[:, k:k + 1], mean_var[:, k, 1:2], LN_EPS, None, ALU.add)\
                    .then_inc(var_ready, 1)

            def layernorm(k, src, dst):
                return dve.tensor_scalar(dst, src, mean_var[:, k, 0:1], inv_std[:, k:k + 1], ALU.subtract, ALU.mult)

            def emit(b, i, e, n=None, local=None, base=None):
                kind = e[0]
                if base is None:
                    base = LINK.before(b, i)
                link_base[0], links[0] = base, 0
                if kind == "norm0":
                    squares(b, e[1], e[2])
                elif kind == "norm1":
                    inverse_rms()
                elif kind == "norm2":
                    normalise(b, e[1], e[2])
                elif kind == "ln1":
                    _, half, t, back = e
                    dve.wait_ge(inv_std_ready, last_ln(b, i, "wo"))
                    w = ADDS.before(b, i)
                    if not (isinstance(w, int) and w == 0):
                        dve.wait_ge(x1_b2_ready, w)
                    link(layernorm(0, z[:, 0, :], x1[:, t % 2, :]))
                    link(dve.tensor_copy(x1_parts[:, t % 2, 0, :], x1[:, t % 2, :]))
                    dve.tensor_tensor(x1_parts[:, t % 2, 1, :], x1[:, t % 2, :], x1_parts[:, t % 2, 0, :],
                                      ALU.subtract).then_inc(x1_ready, 1)
                elif kind == "ln2":
                    t = e[2]
                    dve.wait_ge(inv_std_ready, last_ln(b, i, "f2"))
                    dve.wait_ge(y_out_free[t % 2], stored_before(b, i, t) + 16)
                    layernorm(1, z[:, 1 + t % 2, :], y_out[:, t % 2, :]).then_inc(out_ready, 1)
                elif kind == "copy":
                    u = e[1]
                    dve.wait_ge(attend_done, step_index(b + e[2], u, 0) + UNIT_STEPS[unit_half(u)])
                    dve.tensor_copy(yT_unit[:, :], attended[:, :]).then_inc(yT_copied, 1)
                elif kind == "split":
                    _, half, t, back = e
                    dve.wait_ge(gelu_done, GELUS.before(b, i))
                    dve.wait_ge(side_filled, SIDE.before(b, i))
                    h = hidden[:, t].rearrange("p f c -> p (f c)")
                    parts = h_parts_of(b, t)
                    link(dve.tensor_scalar(parts[:, 0, :], h, h_scale[:, 4:5], None, ALU.mult))
                    dve.scalar_tensor_tensor(parts[:, 1, :], h, h_scale[:, 4:5], parts[:, 0, :],
                                             op0=ALU.mult, op1=ALU.subtract).then_inc(h_split, 1)
                elif kind == "h_sum":
                    dve.wait_ge(b1_loaded, 16)
                    dve.tensor_reduce(h_scale[:, 0:1], b1_col[:, :], AX.X, ALU.max,
                                      apply_absolute_value=True).then_inc(summed, 1)
                elif kind == "t_sum":
                    dve.wait_ge((w1_loaded, w2_loaded)[e[1]], 16)
                    dve.tensor_reduce(tern[:, e[1], 0:1], (w1_in, w2_in)[e[1]].rearrange("p a c -> p (a c)"),
                                      AX.X, ALU.add, apply_absolute_value=True).then_inc(summed, 1)
                elif kind == "t_make":
                    w = e[1]
                    dve.wait_ge(side_drained, SIDE.before(b, i))
                    dve.wait_ge(parts_ready, PAIRS)
                    flat = (w1_in, w2_in)[w].rearrange("p a c -> p (a c)")
                    dst = (w1_tern, w2_tern)[w].rearrange("p a c -> p (a c)")
                    link(dve.tensor_scalar(w_neg, flat, tern[:, w, 3:4], None, ALU.is_lt))
                    dve.scalar_tensor_tensor(dst, flat, tern[:, w, 2:3], w_neg, op0=ALU.is_gt,
                                             op1=ALU.subtract).then_inc(summed, 1)
                if kind not in SIDE_JOBS:
                    return
                if n is None:
                    n = SIDE.before(b, i)
                    local = counted(PLANS[kind_of(b)][:i], SIDE.weigh)
                bank = side[local % SIDE_BANKS]
                bank16 = bank[:, :].bitcast(FP16)
                dve.wait_ge(side_filled, n + 1)
                if kind == "w_qkv":
                    w = e[1]
                    dve.tensor_copy(w_qkvT[:, :, w * DIM:(w + 1) * DIM],
                                    bank[:, :].rearrange("p (k c) -> p k c", k=KT)).then_inc(side_drained, 1)
                elif kind == "w_o":
                    dve.tensor_copy(w_oT[:, :, :].rearrange("p k c -> p (k c)"), bank[:, :])\
                        .then_inc(side_drained, 1)
                elif kind == "b2":
                    dve.tensor_copy(b2_all[:, :], bank[:, 0:DIM]).then_inc(side_drained, 1)
                elif kind == "h_scale":
                    link(dve.tensor_scalar(h_scale[:, 1:2], bank[:, 0:1], float(DIM + 1), None, ALU.add))
                    link(dve.reciprocal(h_scale[:, 2:3], h_scale[:, 1:2]))
                    link(dve.tensor_scalar(h_scale[:, 4:5], h_scale[:, 2:3], 60000.0, 1.0, ALU.mult, ALU.min))
                    link(dve.reciprocal(h_scale[:, 5:6], h_scale[:, 4:5]))
                    dve.sem_inc(side_drained, 1)
                elif kind == "t_mean":
                    m = tern[:, e[1], :]
                    link(dve.tensor_scalar(m[:, 1:2], bank[:, 0:1], 1.0 / (FF * DIM), 1e-8, ALU.mult, ALU.max))
                    dve.tensor_scalar(m[:, 2:3], m[:, 1:2], 0.5, None, ALU.mult)
                    dve.tensor_scalar(m[:, 3:4], m[:, 1:2], -0.5, None, ALU.mult).then_inc(side_drained, 1)
                elif kind == "w1":
                    dve.tensor_copy(w1T[:, e[1], :], bank16).then_inc(side_drained, 1)
                elif kind == "w2":
                    dve.tensor_copy(w2T[:, FT // 2 * e[1]:FT // 2 * (e[1] + 1), :].rearrange("p f c -> p (f c)"),
                                    bank16).then_inc(side_drained, 1)
                elif kind == "fin":
                    u = e[1]
                    hg = u % HGS
                    view = bank[:, :].rearrange("p (t h d) -> p t h d", t=CT, h=GROUP_HEADS)
                    link(dve.reciprocal(inv_den[:, :].rearrange("p (t h) -> p t h", t=CT), view[:, :, :, HEAD_DIM]))
                    dst = y_tok[:, unit_half(u)].rearrange("p t (h d) -> p t h d", d=HEAD_DIM)
                    dve.tensor_tensor(dst[:, :, GROUP_HEADS * hg:GROUP_HEADS * (hg + 1), :],
                                      view[:, :, :, 0:HEAD_DIM],
                                      inv_den[:, :].rearrange("p (t h) -> p t h", t=CT).unsqueeze(3)
                                      .to_broadcast([P, CT, GROUP_HEADS, HEAD_DIM]), ALU.mult)\
                        .then_inc(side_drained, 1)
                elif kind == "prep_q":
                    dve.tensor_copy(qT[:, e[1] % 2].rearrange("p h c -> p (h c)"), bank16).then_inc(side_drained, 1)
                elif kind == "prep_k":
                    dve.tensor_copy(kT[:, e[1] % 2, e[2]].rearrange("p h c -> p (h c)"), bank16)\
                        .then_inc(side_drained, 1)
                elif kind == "xt":
                    dve.tensor_copy(xT[:, e[3]].rearrange("p k c -> p (k c)"), bank[:, 0:DIM])\
                        .then_inc(side_drained, 1)
                elif kind == "qk":
                    dve.tensor_copy(qk_raw[:, e[3], :], bank[:, :]).then_inc(side_drained, 1)
                    dve.wait_ge(side_drained, n + 1)
                elif kind == "v":
                    dve.tensor_copy(values[:, kept_at(b + e[2], 2 * e[1] + e[3], 1), :]
                                    .rearrange("p a c -> p (a c)"), bank[:, 0:DIM]).then_inc(side_drained, 1)
                elif kind == "yt":
                    dve.tensor_copy(yT[:, e[2] % 2].rearrange("p k c -> p (k c)"), bank[:, 0:DIM])\
                        .then_inc(side_drained, 1)
                elif kind == "wo":
                    _, half, t, back = e
                    bb = b + back
                    dve.wait_ge(res_loaded[t % 2], (bb * (TILES // 2) + (CT * half + t) // 2 + 1) * 16)
                    dve.tensor_tensor(z[:, 0, :], bank[:, 0:DIM], x_res[:, t % 2, :], ALU.add)\
                        .then_inc(side_drained, 1)
                    dve.wait_ge(side_drained, n + 1)
                    statistics(0, z[:, 0, :])
                elif kind == "x1t":
                    dve.tensor_copy(x1T[:, e[2] % 2].rearrange("p a k c -> p (a k c)"), bank16[:, 0:2 * DIM])\
                        .then_inc(side_drained, 1)
                elif kind == "f1":
                    _, half, t, back, a = e
                    fs = slice(FT // 2 * a, FT // 2 * (a + 1))
                    dve.tensor_tensor(hidden[:, t, fs, :], bank[:, :].rearrange("p (f t) -> p f t", t=P),
                                      b1_col[:, fs].unsqueeze(2).to_broadcast([P, FT // 2, P]), ALU.add)\
                        .then_inc(side_drained, 1)
                elif kind == "f2":
                    _, half, t, back = e
                    dve.scalar_tensor_tensor(z[:, 1 + t % 2, :], bank[:, 0:DIM], h_scale[:, 5:6],
                                             x1_b2[:, t, :], op0=ALU.mult, op1=ALU.add)\
                        .then_inc(side_drained, 1)
                    dve.wait_ge(side_drained, n + 1)
                    statistics(1, z[:, 1 + t % 2, :])
                assert links[0] == LINKS.get(kind, 0), (kind, links[0])

            def last_ln(b, i, name):
                events = PLANS[kind_of(b)]
                return LN.before(b, max(k for k in range(i) if events[k][0] == name) + 1)

            def stored_before(b, i, t):
                c = Count(lambda e: 16 * int(e[0] == "ln2" and e[2] % 2 == t % 2))
                return c.before(b, i)

            base = 0
            for i, e in enumerate(PROLOGUE):
                n = counted(PROLOGUE[:i], SIDE.weigh)
                emit(0, None, e, n=n, local=n, base=base)
                base += LINKS.get(e[0], 0)
            batches(dve, emit)


def parts_needed(half):
    return PAIRS if half else PAIRS // 2


def emit_prologue(pe, e, i, local, emit):
    if e[0] != "norm":
        emit(0, i, e, events=PROLOGUE, local=local)


_INS = ["L0_attn_x", "L0_attn_w_q", "L0_attn_w_k", "L0_attn_w_v", "L0_attn_w_o",
        "L0_ffn_W1", "L0_ffn_b1", "L0_ffn_W2", "L0_ffn_b2"]


def kernel(**inputs):
    import numpy as np
    import concourse.bacc as bacc
    from concourse.bass_utils import run_bass_kernel_spmd

    nc = bacc.Bacc("TRN2", target_bir_lowering=False, num_devices=1)
    arrays, args = {}, []
    for name in _INS:
        a = np.ascontiguousarray(inputs[name])
        arrays[f"in_{name}"] = a
        args.append(nc.dram_tensor(f"in_{name}", a.shape, mybir.dt.from_np(a.dtype), kind="ExternalInput").ap())
    args.append(nc.dram_tensor("out", (BATCH, SEQ, DIM), FP32, kind="ExternalOutput").ap())
    build(nc, *args)
    r = run_bass_kernel_spmd(nc, [arrays], core_ids=[0])
    return r.results[0]["out"]
```

```python
from contextlib import ExitStack

import concourse.bass as bass
from concourse import mybir

FP32, FP16, INT32 = mybir.dt.float32, mybir.dt.float16, mybir.dt.int32
ACT = mybir.ActivationFunctionType
ALU = mybir.AluOpType
AX = mybir.AxisListType

BATCH, SEQ, DIM = 4, 1024, 256
HEADS, HEAD_DIM, FF = 16, 16, 1024
SOFTCAP = 50.0
RMS_EPS, LN_EPS = 1.1920929e-07, 1e-05
P = 128
TILES = SEQ // P
CHUNK = 512
CT = CHUNK // P
GROUP_HEADS = 4
HGS = HEADS // GROUP_HEADS
UNITS = 2 * HGS
KT = DIM // P
FT = FF // P
GROUP = 1024
SIDE_BANKS = 3

def steps_of(half):
    steps = []
    for kt in range(CT * half):
        steps.append(([[(h, kt, (h % 2) * 512, 512, 0) for h in (2 * g, 2 * g + 1)] for g in range(2)], None))
    d = CT * half
    steps.append(([[(h, d, (h % 2) * 512, 512, 0) for h in (2 * g, 2 * g + 1)] for g in range(2)],
                  (2, 512, 1, 0)))
    steps.append(([[x for h in (2 * g, 2 * g + 1) for x in ((h, d + 1, (h % 2) * 512, 384, 128),
                                                           (h, d + 3, (h % 2) * 512 + 384, 128, 384))]
                   for g in range(2)], (2, 512, 2, 384)))
    steps.append(([[(h, d + 2, (h % 2) * 512 + (h // 2) * 256, 256, 256) for h in range(4)]], (4, 256, 1, 0)))
    return steps


STEPS = [steps_of(0), steps_of(1)]
UNIT_STEPS = [len(s) for s in STEPS]
UNIT_GROUPS = [sum(len(g) for g, _ in s) for s in STEPS]
UNIT_MASKS = [sum(len(g) for g, m in s if m) for s in STEPS]


def before_unit(per_half, u):
    return sum(per_half[v // HGS] if v < UNITS else 0 for v in range(u)) if u < UNITS else HGS * sum(per_half)


GROUP_STEPS = [(u, s) for u in range(UNITS) for s, (gs, _) in enumerate(STEPS[u // HGS]) for _ in gs]
BATCH_STEPS, BATCH_GROUPS, BATCH_MASKS = (HGS * sum(x) for x in (UNIT_STEPS, UNIT_GROUPS, UNIT_MASKS))

SIDE_JOBS = ("w_qkv", "w_o", "b2", "h_scale", "t_mean", "w1", "w2",
             "fin", "prep_q", "prep_k", "xt", "qk", "v", "yt", "wo", "x1t", "f1", "f2")
HALF_JOBS = ("qka", "f2a")


def named(word, kind):
    name, _, sub = word.partition(":")
    where = tuple(int(x) for x in sub)
    if name in ("w_o", "b2", "h_sum", "h_scale", "t_sum", "t_mean", "t_make", "w1", "w2"):
        return (name, *where)
    if name in ("xt", "qka", "qk", "v") and len(where) == 2:
        return (name, where[0], 0, where[1])
    if name in ("norm0", "norm1", "norm2", "low") and len(where) == 1:
        return (name, where[0], 0)
    if len(where) >= 2:
        back = 0 if kind == "last" and where[0] == 0 else -1
        return (name, where[0], back, *where[1:]) if name == "gelu" else (name, *where[:2], back, *where[2:])
    return None


def plan(kind):
    out = []
    if kind == "end":
        last = (UNITS - 1, UNIT_STEPS[1] - 1, -1)
        for word in SLOTS_END.split():
            out.append({"mask": ("mask", *last), "attend": ("attend", *last), "copy": ("copy", UNITS - 1, -1),
                        "fin": ("fin", UNITS - 1, -1)}.get(word) or named(word, kind))
        return out
    for u in range(UNITS):
        half, hg = divmod(u, HGS)
        n = UNIT_STEPS[half]
        post1 = None if kind == "first" and half == 0 else (1 - half, hg, -1 if half == 0 else 0)
        post2 = None if kind == "first" else (half, hg, -1)
        lag = (1 - half, hg - 1, post1[2]) if hg and post1 else \
            (half, CT - 1, -1) if not hg and kind != "first" else None
        before = (u - 1, UNIT_STEPS[(u - 1) // HGS] - 1, 0) if u else (UNITS - 1, UNIT_STEPS[1] - 1, -1)
        if kind == "first" and u == 0:
            before = None
        more = not (kind == "last" and u == UNITS - 1)
        pair = (hg, 1) if half == 1 and kind != "last" else \
            (2 + hg, 0) if half == 0 and kind == "first" and hg < 2 else None
        done = None if u == 0 and kind == "first" else (3, 0) if u == 0 else \
            (hg - 1, 1) if half == 1 and hg and kind != "last" else \
            (1 + hg, 0) if half == 0 and hg in (1, 2) and kind == "first" else None
        slots = SLOTS_FIRST[n * hg:n * hg + n] if kind == "first" and half == 0 else \
            SLOTS_LAST[n * hg:n * hg + n] if kind == "last" and half == 1 else SLOTS_A if half == 0 else SLOTS_B
        for s in range(n):
            out.append(("softmax", u, s))
            nxt = (u, s + 1) if s + 1 < n else (u + 1, 0) if more else None
            prev = (u, s - 1, 0) if s else before
            for word in slots[s].split():
                name, _, sub = word.partition(":")
                if named(word, kind):
                    out.append(named(word, kind))
                elif name in ("scoresa", "scores"):
                    if nxt:
                        out.append((name, *nxt))
                elif name in ("mask", "attend"):
                    if prev:
                        out.append((name, *prev))
                elif name in ("copy", "fin"):
                    if before:
                        out.append((name, before[0], before[2]))
                elif name in ("prep_q", "stage"):
                    if more:
                        out.append((name, u + 1))
                elif name == "prep_k":
                    if more and (sub == "0" or HGS <= u + 1 < UNITS):
                        out.append((name, u + 1, int(sub)))
                elif name in ("xt", "qka", "qk", "v"):
                    if pair:
                        out.append((name, *pair, int(sub)))
                elif name in ("norm0", "norm1", "norm2"):
                    if pair:
                        out.append((name, *pair))
                elif name == "low":
                    if done:
                        out.append((name, *done))
                elif name in ("yt", "wo", "ln1", "add_b2"):
                    if post1:
                        out.append((name, *post1))
                elif name == "x1t":
                    if lag:
                        out.append((name, *lag))
                elif name == "f1":
                    if lag:
                        out.append((name, *lag, int(sub)))
                elif name in ("split", "f2a", "f2", "ln2"):
                    if post2:
                        out.append((name, *post2))
                else:
                    assert name == "gelu"
                    if hg == 0 and post2:
                        out.append((name, half, -1, 0, CT))
    return out


SLOTS_A = [
    "x1t prep_q scoresa scores f1:0 mask xt:0 copy stage attend f1:1 xt:1 low fin prep_k:0 qka:0 qk:0",
    "prep_k:1 mask qka:1 qk:1 scoresa scores yt gelu v:1 attend norm0 split",
    "mask wo norm1 v:0 norm2 f2a ln1 f2 ln2 scoresa scores add_b2 attend",
]
SLOTS_B = [
    "x1t mask attend xt:0 xt:1 f1:0 f1:1 scoresa scores copy gelu",
    "split qka:0 qk:0 qka:1 qk:1 low scoresa scores fin attend yt",
    "norm0 attend f2a scoresa scores f2 v:1 wo ln2 stage",
    "scoresa scores norm1 ln1 v:0 attend",
    "norm2 scoresa scores add_b2 attend prep_q",
    "scoresa mask scores attend prep_k:0",
    "prep_k:1 mask attend scoresa scores",
]
SLOTS_FIRST = [
    "mask xt:20 attend xt:21 scoresa scores qka:20 qk:20",
    "prep_q mask v:20 qka:21 qk:21 scoresa scores prep_k:0 stage v:21 norm0:2 attend w_o",
    "b2 norm1:2 mask norm2:2 low:2 scoresa scores attend",
    "prep_q xt:30 xt:31 scoresa scores qka:30 qk:30 mask copy attend v:30",
    "mask scoresa scores fin qka:31 qk:31 stage norm0:3 prep_k:0 attend",
    "norm1:3 mask norm2:3 low:3 attend v:31 scoresa scores",
    "prep_q scoresa scores mask copy prep_k:0 attend t_sum:0 t_mean:0 t_make:0",
    "scoresa scores t_sum:1 mask attend stage h_sum h_scale",
    "w1:0 fin scoresa scores mask attend w1:1",
    "prep_q scoresa scores mask copy attend t_mean:1",
    "scoresa scores mask stage prep_k:0 t_make:1 fin attend",
    "mask prep_k:1 w2:0 scoresa scores w2:1 attend",
]
SLOTS_LAST = [
    "x1t:13 mask f1:130 scoresa scores stage copy f1:131 attend gelu:104 fin",
    "attend scoresa scores",
    "split:10 yt:00 attend yt:01 scoresa scores f2a:10 f2:10 wo:00 ln2:10 split:11",
    "ln1:00 attend add_b2:00 scoresa scores wo:01",
    "f2a:11 f2:11 ln2:11 attend prep_q scoresa scores",
    "ln1:01 scoresa scores prep_k:0 split:12 mask attend x1t:00",
    "prep_k:1 mask add_b2:01 attend scoresa scores",
    "f1:000 scoresa scores mask stage copy f2a:12 f2:12 attend",
    "yt:02 scoresa scores attend wo:02 f1:001 x1t:01",
    "attend split:13 scoresa scores yt:03 ln2:12",
    "scoresa scores attend fin ln1:02 f2a:13 f2:13 wo:03",
    "scoresa scores x1t:02 attend add_b2:02 ln2:13 f1:010 prep_q",
    "scoresa scores prep_k:0 mask ln1:03 attend",
    "prep_k:1 mask attend scoresa scores add_b2:03 f1:011",
    "mask copy scoresa scores attend f1:020",
    "fin attend scoresa scores x1t:03 stage f1:021",
    "f1:030 attend f1:031 scoresa scores",
    "scoresa scores attend",
    "scoresa scores gelu:004 attend",
    "prep_q scoresa scores prep_k:0 mask prep_k:1 attend split:00",
    "scoresa scores mask attend f2a:00 f2:00",
    "copy scoresa scores mask attend",
    "split:01 attend ln2:00 scoresa scores fin",
    "attend scoresa scores f2a:01 f2:01",
    "attend ln2:01 scoresa scores split:02",
    "attend scoresa scores f2a:02 f2:02 ln2:02",
    "mask attend scoresa scores",
    "mask attend split:03 f2a:03 f2:03 ln2:03 scoresa scores",
]
SLOTS_END = (
    "mask attend copy fin yt:10 yt:11 wo:10 ln1:10 yt:12 add_b2:10 wo:11 x1t:10 ln1:11 add_b2:11 "
    "wo:12 f1:100 x1t:11 f1:101 ln1:12 gelu:101 f1:110 yt:13 split:10 wo:13 f1:111 gelu:111 x1t:12 "
    "ln1:13 f2a:10 f2:10 add_b2:12 x1t:13 f1:120 add_b2:13 split:11 f1:121 ln2:10 f1:130 gelu:121 "
    "f2a:11 f2:11 split:12 f1:131 ln2:11 gelu:131 split:13 f2a:12 f2:12 ln2:12 f2a:13 f2:13 ln2:13"
)
PLANS = {k: plan(k) for k in ("first", "middle", "last", "end")}
PROLOGUE = ([("xt", 0, 0, 0), ("xt", 0, 0, 1)] + [("w_qkv", w) for w in range(3)]
            + [("qk", 0, 0, 0), ("qk", 0, 0, 1), ("first_norm", 0), ("v", 0, 0, 0), ("v", 0, 0, 1),
               ("xt", 1, 0, 0), ("xt", 1, 0, 1), ("qk", 1, 0, 0), ("qk", 1, 0, 1), ("first_norm", 1),
               ("high", 0), ("low", 0, 0), ("v", 1, 0, 0), ("v", 1, 0, 1), ("high", 1), ("low", 1, 0)]
            + [("prep_q", 0), ("prep_k", 0, 0), ("scores", 0, 0)])
LINKS = {"fin": 1, "norm0": 2, "norm1": 8, "norm2": 4, "first_norm": 12, "wo": 2, "ln1": 2, "f2": 2,
         "split": 1, "h_scale": 4, "t_mean": 1, "t_make": 1}
PAIRS = TILES // 2


def kind_of(b):
    return {0: "first", BATCH - 1: "last", BATCH: "end"}.get(b, "middle") if isinstance(b, int) else "middle"


def counted(events, weigh):
    return sum(weigh(e) for e in events)


class Count:

    def __init__(self, weigh):
        self.weigh = weigh
        self.prologue = counted(PROLOGUE, weigh)
        self.first = counted(PLANS["first"], weigh)
        self.middle = counted(PLANS["middle"], weigh)
        self.last = counted(PLANS["last"], weigh)

    def batch(self, b):
        if isinstance(b, int):
            done = [0, self.first]
            for _ in range(1, BATCH - 1):
                done.append(done[-1] + self.middle)
            done.append(done[-1] + self.last)
            return self.prologue + done[b]
        return b * self.middle + (self.prologue + self.first - self.middle)

    def before(self, b, i):
        return self.batch(b) + counted(PLANS[kind_of(b)][:i], self.weigh)


def of(*names):
    return lambda e: int(e[0] in names)


SIDE = Count(of(*SIDE_JOBS))
LINK = Count(lambda e: LINKS.get(e[0], 0))
PAIR = Count(of("low"))
GELUS = Count(lambda e: e[4] if e[0] == "gelu" else 0)
LN = Count(of("wo", "f2"))
OUTS = Count(of("ln2"))
LN1S = Count(of("ln1"))
ADDS = Count(of("add_b2"))
SPLITS = Count(of("split"))
SUMS = Count(of("h_sum", "t_sum", "t_make"))


def build(nc, x, w_q, w_k, w_v, w_o, W1, b1, W2, b2, out):
    x_t = x.rearrange("b (t p) d -> p (b t) d", p=P)
    out_t = out.rearrange("b (t p) d -> p (b t) d", p=P)
    ctx = ExitStack()
    with ctx:
        def sb(name, shape, dt=FP32):
            return ctx.enter_context(nc.sbuf_tensor(name, shape, dt))

        def sem(name):
            return ctx.enter_context(nc.semaphore(name))

        w_qkvT = sb("w_qkvT", [P, KT, 3 * DIM])
        w_oT = sb("w_oT", [P, KT, DIM])
        w1T = sb("w1T", [P, KT, FF], FP16)
        w2T = sb("w2T", [P, FT, DIM], FP16)
        b1_col = sb("b1_col", [P, FT])
        b2_row = sb("b2_row", [1, DIM])
        b2_all = sb("b2_all", [P, DIM])
        ident = sb("ident", [P, P])
        ident16 = sb("ident16", [P, P], FP16)
        ones = sb("ones", [P, P])
        minus_half = sb("minus_half", [P, 1])
        tern = sb("tern", [P, 2, 4])
        h_scale = sb("h_scale", [P, 6])
        x_in = sb("x_in", [P, 2, 2, DIM])
        xT = sb("xT", [P, 2, KT, P])
        qk_raw = sb("qk_raw", [P, 2, 2 * DIM])
        qk_norm = sb("qk_norm", [P, 2, 2 * DIM])
        ssq = sb("ssq", [P, 64])
        rms = sb("rms", [P, 2, 64])
        newton = sb("newton", [P, 64])
        qk_parts = sb("qk_parts", [P, 2, 2 * TILES, HEADS, 4 * HEAD_DIM], FP16)
        values = sb("values", [P, 2 * TILES, DIM])
        qT = sb("qT", [P, 2, 2, CHUNK], FP16)
        kT = sb("kT", [P, 2, 2, 2, CHUNK], FP16)
        v_unit = sb("v_unit", [P, 2, TILES, GROUP_HEADS, 2 * HEAD_DIM])
        capped = sb("capped", [P, 2, GROUP])
        probs = sb("probs", [P, 4, GROUP])
        yT_unit = sb("yT_unit", [P, CHUNK])
        inv_den = sb("inv_den", [P, CT * GROUP_HEADS])
        y_tok = sb("y_tok", [P, 2, CT, DIM])
        yT = sb("yT", [P, 2, KT, P])
        x_res = sb("x_res", [P, 2, DIM])
        z = sb("z", [P, 3, DIM])
        stats = sb("stats", [P, 6])
        mean_var = sb("mean_var", [P, 2, 2])
        var_eps = sb("var_eps", [P, 2])
        inv_std = sb("inv_std", [P, 2])
        x1 = sb("x1", [P, 2, DIM])
        x1_parts = sb("x1_parts", [P, 2, 2, DIM], FP16)
        x1_b2 = sb("x1_b2", [P, CT, DIM])
        x1T = sb("x1T", [P, 2, 2, KT, P], FP16)
        hidden = sb("hidden", [P, CT, FT, P])
        h_parts = sb("h_parts", [P, 2, FT * P], FP16)
        y_out = sb("y_out", [P, 2, DIM])
        w_in = capped[:, :, :].rearrange("p a (w k d) -> p (a w) k d", k=KT, d=DIM)
        w_o_in = y_out[:, :, :]
        room = hidden[:, :, :, :].rearrange("p t f c -> p (t f c)")
        w1_in = room[:, 0:FF * KT].rearrange("p (f d) -> p f d", d=DIM)
        w2_in = room[:, FF * KT:2 * FF * KT].rearrange("p (o f) -> p o f", f=FF)
        w1_tern = x1_b2[:, :, :].rearrange("p t d -> p (t d)").bitcast(FP16)\
            .rearrange("p (f d) -> p f d", d=DIM)
        w2_tern = h_parts[:, :, :]
        w_neg = qk_norm[:, :, :].rearrange("p t c -> p (t c)").bitcast(FP16)
        first_raw = (qk_raw, probs[:, 0, :].rearrange("p (t c) -> p t c", t=2))
        first_norms = (qk_norm, probs[:, 1, :].rearrange("p (t c) -> p t c", t=2))
        h_parts_odd = probs[:, 0, :].bitcast(FP16).rearrange("p (k f) -> p k f", k=2)

        scores = ctx.enter_context(nc.psum_tensor("scores", [P, 2, GROUP], FP32))
        attended = ctx.enter_context(nc.psum_tensor("attended", [P, CHUNK], FP32))
        side = [ctx.enter_context(nc.psum_tensor(f"side{i}", [P, 512], FP32)) for i in range(SIDE_BANKS)]

        w_loaded = sem("w_loaded")
        w_o_loaded = sem("w_o_loaded")
        w1_loaded = sem("w1_loaded")
        w2_loaded = sem("w2_loaded")
        b1_loaded = sem("b1_loaded")
        b2_loaded = sem("b2_loaded")
        x_loaded = [sem("x_loaded0"), sem("x_loaded1")]
        res_loaded = [sem("res_loaded0"), sem("res_loaded1")]
        y_out_free = [sem("y_out_free0"), sem("y_out_free1")]
        consts = sem("consts")
        consts_step = sem("consts_step")
        summed = sem("summed")
        h_split = sem("h_split")
        side_filled = sem("side_filled")
        side_drained = sem("side_drained")
        linked = sem("linked")
        first_normed = sem("first_normed")
        first_high = sem("first_high")
        first_low = sem("first_low")
        high_ready = sem("high_ready")
        parts_ready = sem("parts_ready")
        v_staged = sem("v_staged")
        scores_ready = sem("scores_ready")
        capped_ready = sem("capped_ready")
        probs_ready = sem("probs_ready")
        masked = sem("masked")
        attend_done = sem("attend_done")
        yT_copied = sem("yT_copied")
        var_ready = sem("var_ready")
        inv_std_ready = sem("inv_std_ready")
        x1_ready = sem("x1_ready")
        x1_b2_ready = sem("x1_b2_ready")
        gelu_done = sem("gelu_done")
        out_ready = sem("out_ready")
        held = [sem(f"held{n}") for n in range(3)]

        block = ctx.enter_context(nc.Block())

        def batches(eng, emit):
            for i, e in enumerate(PLANS["first"]):
                emit(0, i, e)
            with eng.Fori(1, BATCH - 1) as b:
                for i, e in enumerate(PLANS["middle"]):
                    emit(b, i, e)
            for i, e in enumerate(PLANS["last"]):
                emit(BATCH - 1, i, e)
            for i, e in enumerate(PLANS["end"]):
                emit(BATCH, i, e)

        def hold(eng, semaphore, value):
            eng.wait_ge(semaphore, value)
            if not isinstance(value, int):
                eng.sem_inc(held[[nc.vector, nc.tensor, nc.gpsimd].index(eng)], 1)

        def tiles_at(b, first, n):
            return bass.ds(b * TILES + first, n)

        def kept_at(b, first, n):
            at = (b & 1) * TILES + first
            return slice(at, at + n) if isinstance(at, int) else bass.ds(at, n)

        def part_slots(b, t, which):
            tile = qk_parts[:, which, kept_at(b, t, 1)].rearrange("p a h c -> p (a h) c")
            if which == 0:
                slots = tile.rearrange("p h (r k d) -> p h r k d", r=2, k=2)
                return slots[:, :, :, 0, :], slots[:, :, :, 1, :]
            slots = tile.rearrange("p h (k r d) -> p h k r d", r=2, k=2)
            return slots[:, :, 0, :, :], slots[:, :, 1, :, :]

        def head_view(t, which, norm=None):
            norm = qk_norm if norm is None else norm
            return norm[:, t, which * DIM:(which + 1) * DIM].rearrange("p (h d) -> p h d", d=HEAD_DIM)\
                .unsqueeze(2).to_broadcast([P, HEADS, 2, HEAD_DIM])

        def group_index(b, u, s, g):
            half = min(u, UNITS - 1) // HGS if u < UNITS else 0
            in_unit = sum(len(x) for x, _ in STEPS[half][:s]) + g
            return b * BATCH_GROUPS + before_unit(UNIT_GROUPS, u) + in_unit

        def step_index(b, u, s):
            return b * BATCH_STEPS + before_unit(UNIT_STEPS, u) + s

        def turn(u, s, g, buffers):
            return group_index(0, u % UNITS, s, g) % buffers

        def step_before(b, u, s, g, n):
            k = group_index(0, u % UNITS, s, g) - n
            if k < 0 and isinstance(b, int) and b == 0:
                return None
            uu, ss = GROUP_STEPS[k]
            return step_index(b - int(k < 0), uu, ss) + 1

        def h_parts_of(b, t):
            return h_parts_odd if isinstance(b, int) and b == BATCH and t % 2 else h_parts

        def side_jobs_to(event):
            return counted(PROLOGUE[:PROLOGUE.index(event) + 1], SIDE.weigh)

        def unit_half(u):
            return (u % UNITS) // HGS

        @block.sync
        def _(sp):
            def load_pair(b, pair):
                sp.dma_start(x_in[:, pair % 2], x_t[:, tiles_at(b, 2 * pair, 2), :]).then_inc(x_loaded[pair % 2], 16)

            def load_residual(b, half, t):
                sp.dma_start(x_res[:, t % 2], x_t[:, b * TILES + CT * half + t, :] if isinstance(b, int)
                             else x_t[:, bass.ds(b * TILES + CT * half + t, 1), :].rearrange("p a d -> p (a d)"))\
                    .then_inc(res_loaded[t % 2], 16)

            load_pair(0, 0)
            load_pair(0, 1)
            load_residual(0, 0, 0)
            load_residual(0, 0, 1)
            for p in (0, 1):
                sp.wait_ge(side_drained, side_jobs_to(("xt", p, 0, 1)))
                load_pair(0, p + 2)

            def emit(b, i, e):
                if e[0] == "xt" and e[3] == 1:
                    pair, ahead = e[1], e[2]
                    if ahead == 0 or pair + 2 < PAIRS:
                        sp.wait_ge(side_drained, SIDE.before(b, i) + 1)
                        load_pair(b + 1, pair - 2 if ahead == 0 else pair + 2)
                if i == 0 and kind_of(b) == "middle":
                    sp.wait_ge(side_drained, SIDE.batch(b))
                    load_pair(b + 1, 0)
                    load_pair(b + 1, 1)
                if e[0] == "wo":
                    _, half, t, back = e
                    sp.wait_ge(side_drained, SIDE.before(b, i) + 1)
                    nb = b + back
                    if t + 2 < CT:
                        load_residual(nb, half, t + 2)
                    elif half == 0:
                        load_residual(nb, 1, t - 2)
                    elif not (isinstance(b, int) and b == BATCH):
                        load_residual(nb + 1, 0, t - 2)
                if e[0] == "ln2":
                    _, half, t, back = e
                    sp.wait_ge(out_ready, OUTS.before(b, i) + 1)
                    nb = b + back
                    dst = out_t[:, bass.ds(nb * TILES + CT * half + t, 1), :].rearrange("p a d -> p (a d)") \
                        if not isinstance(nb, int) else out_t[:, nb * TILES + CT * half + t, :]
                    sp.dma_start(dst, y_out[:, t % 2]).then_inc(y_out_free[t % 2], 16)

            for par in range(2):
                sp.sem_inc(y_out_free[par], 16)
            batches(sp, emit)
            for par in range(2):
                sp.wait_ge(y_out_free[par], 16 + 16 * BATCH * TILES // 2)

        @block.gpsimd
        def _(pool):
            pool.memset(ident[:, :], 0.0).then_inc(consts_step, 1)
            pool.memset(ident16[:, :], 0.0).then_inc(consts_step, 1)
            pool.wait_ge(consts_step, 2)
            for m in (ident, ident16):
                pool.affine_select(out=m[:, :], in_=m[:, :], compare_op=ALU.not_equal, fill=1.0, base=0,
                                   pattern=[[-1, P]], channel_multiplier=1).then_inc(consts, 1)
            pool.memset(ones[:, :], 1.0).then_inc(consts, 1)
            pool.memset(minus_half[:, :], -0.5).then_inc(consts, 1)
            pool.memset(v_unit[:, :, :, :, HEAD_DIM:], 1.0).then_inc(consts, 1)
            pool.wait_ge(consts, 5)

            def low_parts(b, pair, ahead):
                for t in range(2):
                    for which in range(2):
                        high, low = part_slots(b + ahead, 2 * pair + t, which)
                        ins = pool.tensor_tensor(low, head_view(t, which), high, ALU.subtract)
                ins.then_inc(parts_ready, 1)

            def stage_values(b, u):
                n = TILES if unit_half(u) else CT
                hg = u % HGS
                bb = b + u // UNITS
                src = values[:, kept_at(bb, 0, n), GROUP_HEADS * HEAD_DIM * hg:GROUP_HEADS * HEAD_DIM * (hg + 1)]
                pool.tensor_copy(v_unit[:, u % 2, 0:n, :, 0:HEAD_DIM],
                                 src.rearrange("p t (h d) -> p t h d", d=HEAD_DIM)).then_inc(v_staged, 1)

            pool.wait_ge(first_high, 4)
            low_parts(0, 0, 0)
            pool.wait_ge(first_high, 6)
            for which in range(2):
                high, low = part_slots(0, 2, which)
                ins = pool.tensor_tensor(low, head_view(0, which, first_norms[1]), high, ALU.subtract)
            ins.then_inc(parts_ready, 1)
            pool.wait_ge(side_drained, side_jobs_to(("v", 1, 0, 1)))
            stage_values(0, 0)

            def emit(b, i, e):
                if e[0] == "low":
                    pool.wait_ge(high_ready, PAIR.before(b, i) + 1 - PAIR.prologue)
                    low_parts(b, e[1], e[2])
                elif e[0] == "stage":
                    u = e[1]
                    pool.wait_ge(side_drained, SIDE.before(b, i))
                    if not (isinstance(b, int) and b == 0 and u < 2):
                        hold(pool, attend_done, step_index(b, u - 1, 0))
                    stage_values(b, u)
                elif e[0] in ("wo", "f2"):
                    pool.wait_ge(var_ready, LN.before(b, i) + 1)
                    k = int(e[0] == "f2")
                    pool.tensor_tensor(inv_std[:, k:k + 1], var_eps[:, k:k + 1], minus_half[:, :], ALU.pow)\
                        .then_inc(inv_std_ready, 1)
                elif e[0] == "add_b2":
                    t = e[2]
                    pool.wait_ge(x1_ready, LN1S.before(b, i))
                    pool.wait_ge(side_drained, SIDE.before(b, i))
                    pool.tensor_tensor(x1_b2[:, t, :], x1[:, t % 2, :], b2_all[:, :], ALU.add)\
                        .then_inc(x1_b2_ready, 1)
                elif e[0] == "mask":
                    _, u, s, back = e
                    groups, diag = STEPS[unit_half(u)][s]
                    if diag:
                        n, stride, m, inner = diag
                        for g in range(len(groups)):
                            hold(pool, probs_ready, group_index(b + back, u, s, g) + 1)
                            buf = probs[:, turn(u, s, g, 4), :]
                            for k in range(m):
                                view = buf.rearrange("p (h c) -> p h c", c=stride)[:, :, k * inner:k * inner + P]
                                ins = pool.affine_select(out=view, in_=view, compare_op=ALU.is_ge, fill=0.0,
                                                         base=0, pattern=[[0, n], [1, P]], channel_multiplier=-1)
                            ins.then_inc(masked, 1)

            batches(pool, emit)

        @block.scalar
        def _(act):
            for i, w in enumerate((w_q, w_k, w_v)):
                act.dma_start(w_in[:, i], w.rearrange("(o p) d -> p o d", p=P)).then_inc(w_loaded, 16)
            act.dma_start(w_o_in, w_o.rearrange("(o p) d -> p o d", p=P)).then_inc(w_o_loaded, 16)
            act.dma_start(b2_row[0:1, :], b2.rearrange("(a d) -> a d", a=1)).then_inc(b2_loaded, 16)
            with nc.allow_non_contiguous_dma(reason="1024 biases, once"):
                act.dma_start(b1_col[:, :], b1.rearrange("(f p) -> p f", p=P)).then_inc(b1_loaded, 16)
            act.dma_start(w1_in, W1.rearrange("(f p) d -> p f d", p=P)).then_inc(w1_loaded, 16)
            act.dma_start(w2_in, W2.rearrange("(o p) f -> p o f", p=P)).then_inc(w2_loaded, 16)

            def emit(b, i, e):
                if e[0] == "softmax":
                    _, u, s = e
                    groups, _ = STEPS[unit_half(u)][s]
                    for g in range(len(groups)):
                        n = group_index(b, u, s, g)
                        buf = turn(u, s, g, 2)
                        if not (isinstance(n, int) and n < 2):
                            act.wait_ge(probs_ready, n - 1)
                        act.wait_ge(scores_ready, n + 1)
                        act.activation(capped[:, buf, :], scores[:, buf, :], ACT.Tanh,
                                       scale=1.0 / (SOFTCAP * HEAD_DIM ** 0.5)).then_inc(capped_ready, 1)
                    for g in range(len(groups)):
                        n = group_index(b, u, s, g)
                        used = step_before(b, u, s, g, 4)
                        if used is not None:
                            act.wait_ge(attend_done, used)
                        act.wait_ge(capped_ready, n + 1)
                        act.activation(probs[:, turn(u, s, g, 4), :], capped[:, turn(u, s, g, 2), :], ACT.Exp,
                                       scale=SOFTCAP).then_inc(probs_ready, 1)
                elif e[0] == "gelu":
                    _, half, back, first, n = e
                    act.wait_ge(side_drained, SIDE.before(b, i))
                    for t in range(first, first + n):
                        h = hidden[:, t].rearrange("p f t -> p (f t)")
                        act.activation(h, h, ACT.Gelu).then_inc(gelu_done, 1)

            for i, e in enumerate(PROLOGUE):
                if e[0] == "high":
                    p = e[1]
                    act.wait_ge(first_normed, p + 1)
                    for t in range(2):
                        for which in range(2):
                            high, _ = part_slots(0, 2 * p + t, which)
                            act.activation(high, head_view(t, which, first_norms[p]), ACT.Copy)\
                                .then_inc(first_high, 1)
                if e[0] not in SIDE_JOBS:
                    continue
                n = counted(PROLOGUE[:i], SIDE.weigh)
                bank = side[n % SIDE_BANKS]
                bank16 = bank[:, :].bitcast(FP16)
                act.wait_ge(side_filled, n + 1)
                if e[0] == "xt":
                    ins = act.activation(xT[:, e[3]].rearrange("p k c -> p (k c)"), bank[:, 0:DIM], ACT.Copy)
                elif e[0] == "w_qkv":
                    ins = act.activation(w_qkvT[:, :, e[1] * DIM:(e[1] + 1) * DIM],
                                         bank[:, :].rearrange("p (k c) -> p k c", k=KT), ACT.Copy)
                elif e[0] == "qk":
                    act.activation(first_raw[e[1]][:, e[3], :], bank[:, :], ACT.Copy)
                    ins = act.activation(first_norms[e[1]][:, e[3], :], bank[:, :], ACT.Square)
                elif e[0] == "v":
                    ins = act.activation(values[:, 2 * e[1] + e[3], :], bank[:, 0:DIM], ACT.Copy)
                elif e[0] == "prep_q":
                    ins = act.activation(qT[:, 0].rearrange("p h c -> p (h c)"), bank16, ACT.Copy)
                else:
                    ins = act.activation(kT[:, 0, 0].rearrange("p h c -> p (h c)"), bank16, ACT.Copy)
                ins.then_inc(side_drained, 1)
            batches(act, emit)

        @block.tensor
        def _(pe):
            pe.wait_ge(consts, 5)

            def scores_step(b, u, s, first=0, last=2):
                par = u % 2
                groups, _ = STEPS[unit_half(u)][s]
                for g, pieces in list(enumerate(groups))[first:last]:
                    n, buf = group_index(b, u, s, g), turn(u, s, g, 2)
                    if not (isinstance(n, int) and n < 2):
                        pe.wait_ge(capped_ready, n - 1)
                    for h, kt, off, width, q0 in pieces:
                        r = 64 * (h % 2)
                        ins = pe.matmul(scores[:, buf, off:off + width],
                                        kT[r:r + 64, par, kt // CT, h // 2, (kt % CT) * P:(kt % CT + 1) * P],
                                        qT[r:r + 64, par, h // 2, q0:q0 + width], start=True, stop=True)
                    ins.then_inc(scores_ready, 1)

            def attend_step(b, u, s, back):
                half, par = unit_half(u), u % 2
                b = b + back
                groups, diag = STEPS[half][s]
                if s == 0:
                    pe.wait_ge(v_staged, b * UNITS + u + 1)
                    if not (isinstance(b, int) and b == 0 and u == 0):
                        pe.wait_ge(yT_copied, b * UNITS + u)
                if diag:
                    in_unit = sum(len(x) for x, m in STEPS[half][:s + 1] if m)
                    pe.wait_ge(masked, b * BATCH_MASKS + before_unit(UNIT_MASKS, u) + in_unit)
                else:
                    pe.wait_ge(probs_ready, group_index(b, u, s, len(groups) - 1) + 1)
                pieces = [(g, x) for g, xs in enumerate(groups) for x in xs]
                pieces.sort(key=lambda gx: (gx[1][1], gx[1][0]))
                for g, (h, kt, off, width, q0) in pieces:
                    ins = pe.matmul(attended[32 * h:32 * h + 32, q0:q0 + width], v_unit[:, par, kt, h, :],
                                    probs[:, turn(u, s, g, 4), off:off + width], start=(s == 0),
                                    stop=(s == UNIT_STEPS[half] - 1), skip_group_check=True)
                ins.then_inc(attend_done, 1)

            def side_bank(b, local, in_prologue, own_wait):
                base = 0 if in_prologue else SIDE.batch(b)
                drained = base + max(local - SIDE_BANKS + 1, 0)
                if own_wait:
                    hold(pe, side_drained, drained)
                elif not (isinstance(drained, int) and drained == 0):
                    pe.wait_ge(side_drained, drained)
                return side[local % SIDE_BANKS]

            def emit(b, i, e, events=None, local=None):
                kind = e[0]
                if local is None:
                    local = counted(PLANS[kind_of(b)][:i], SIDE.weigh)
                if kind in ("scoresa", "scores"):
                    _, u, s = e
                    groups = len(STEPS[unit_half(u)][s][0])
                    if s == 0 and kind == "scoresa":
                        pe.wait_ge(side_drained, prep_done(b, i, u))
                    scores_step(b, u, s, *((0, groups - 1) if kind == "scoresa" else (groups - 1, groups)))
                elif kind == "attend":
                    attend_step(b, *e[1:])
                if kind not in SIDE_JOBS + HALF_JOBS:
                    return
                if kind == "fin":
                    pe.wait_ge(yT_copied, (b + e[2]) * UNITS + e[1] + 1)
                elif kind == "w_qkv":
                    pe.wait_ge(w_loaded, 48)
                elif kind == "w_o":
                    pe.wait_ge(w_o_loaded, 16)
                elif kind == "b2":
                    pe.wait_ge(b2_loaded, 16)
                elif kind in ("h_scale", "t_mean", "w1", "w2"):
                    pe.wait_ge(summed, SUMS.before(b, i))
                elif kind in ("prep_q", "prep_k"):
                    u = e[1]
                    bb = b + u // UNITS
                    need = parts_needed(unit_half(u))
                    pe.wait_ge(parts_ready, (b + u // UNITS) * PAIRS + need)
                    if events is not None:
                        pe.wait_ge(first_low, 1)
                elif kind == "xt":
                    pair, ahead = e[1], e[2]
                    pe.wait_ge(x_loaded[pair % 2], ((b + ahead) * (PAIRS // 2) + pair // 2 + 1) * 16)
                elif kind == "x1t":
                    ln1 = ("ln1", *e[1:])
                    pe.wait_ge(x1_ready, done(b, i, ln1, LN1S) if ln1 in PLANS[kind_of(b)][:i]
                               else LN1S.batch(b))
                bank = side_bank(b, local, events is not None, kind in ("prep_q", "prep_k"))
                bank16 = bank[:, :].bitcast(FP16)
                if kind in ("w_qkv", "w_o"):
                    src = w_o_in if kind == "w_o" else w_in[:, e[1]]
                    for kt in range(KT):
                        for o in range(KT):
                            ins = pe.transpose(bank[:, (kt * KT + o) * P:(kt * KT + o + 1) * P],
                                               src[:, o, kt * P:(kt + 1) * P], ident[:, :])
                elif kind == "b2":
                    ins = pe.matmul(bank[:, 0:DIM], ones[0:1, :], b2_row[0:1, :], start=True, stop=True)
                elif kind in ("h_scale", "t_mean"):
                    src = h_scale[:, 0:1] if kind == "h_scale" else tern[:, e[1], 0:1]
                    ins = pe.matmul(bank[:, 0:1], ones[:, :], src, start=True, stop=True)
                elif kind == "w1":
                    for f in range(FT):
                        ins = pe.transpose(bank16[:, f * P:(f + 1) * P],
                                           w1_tern[:, f, e[1] * P:(e[1] + 1) * P], ident16[:, :])
                elif kind == "w2":
                    for k in range(FT):
                        f, o = FT // 2 * e[1] + k // 2, k % 2
                        ins = pe.transpose(bank16[:, k * P:(k + 1) * P], w2_tern[:, o, f * P:(f + 1) * P],
                                           ident16[:, :])
                elif kind == "fin":
                    for t in range(CT):
                        ins = pe.transpose(bank[:, t * P:(t + 1) * P], yT_unit[:, t * P:(t + 1) * P], ident[:, :])
                elif kind in ("prep_q", "prep_k"):
                    is_k = kind == "prep_k"
                    first = CT * e[2] if is_k else CT * unit_half(u)
                    for hp in range(2):
                        for t in range(CT):
                            h0 = GROUP_HEADS * (u % HGS) + 2 * hp
                            src = qk_parts[:, int(is_k), kept_at(bb, first + t, 1), h0:h0 + 2, :]\
                                .rearrange("p a h c -> p (a h c)")
                            ins = pe.transpose(bank16[:, hp * CHUNK + t * P:hp * CHUNK + (t + 1) * P],
                                               src, ident16[:, :])
                elif kind == "xt":
                    t = e[3]
                    for kt in range(KT):
                        ins = pe.transpose(bank[:, kt * P:(kt + 1) * P],
                                           x_in[:, e[1] % 2, t, kt * P:(kt + 1) * P], ident[:, :])
                elif kind in ("qka", "qk", "v"):
                    t = e[3]
                    pe.wait_ge(side_drained, xt_done(b, i, e, events))
                    c0, c1 = (0, 2 * DIM) if kind != "v" else (2 * DIM, 3 * DIM)
                    for kt in {"qka": [0], "qk": [1] if events is None else [0, 1], "v": [0, 1]}[kind]:
                        ins = pe.matmul(bank[:, 0:c1 - c0], xT[:, t, kt, :], w_qkvT[:, kt, c0:c1],
                                        start=(kt == 0), stop=(kt == KT - 1))
                elif kind == "yt":
                    _, half, t, back = e
                    pe.wait_ge(side_drained, last_before(b, i, "fin"))
                    for kt in range(KT):
                        ins = pe.transpose(bank[:, kt * P:(kt + 1) * P],
                                           y_tok[:, half, t, kt * P:(kt + 1) * P], ident[:, :])
                elif kind == "wo":
                    pe.wait_ge(side_drained, done(b, i, ("yt", *e[1:])))
                    for kt in range(KT):
                        ins = pe.matmul(bank[:, 0:DIM], yT[:, e[2] % 2, kt, :], w_oT[:, kt, :], start=(kt == 0),
                                        stop=(kt == KT - 1))
                elif kind == "x1t":
                    for part in range(2):
                        for kt in range(KT):
                            c = (part * KT + kt) * P
                            ins = pe.transpose(bank16[:, c:c + P], x1_parts[:, e[2] % 2, part, kt * P:(kt + 1) * P],
                                               ident16[:, :])
                elif kind == "f1":
                    pe.wait_ge(side_drained, done(b, i, ("x1t", *e[1:4])))
                    for f in range(FT // 2):
                        ft = FT // 2 * e[4] + f
                        for k in range(2 * KT):
                            ins = pe.matmul(bank[:, f * P:(f + 1) * P], w1T[:, k % KT, ft * P:(ft + 1) * P],
                                            x1T[:, e[2] % 2, k // KT, k % KT, :],
                                            start=(k == 0), stop=(k == 2 * KT - 1))
                elif kind in ("f2a", "f2"):
                    _, half, t, back = e
                    pe.wait_ge(h_split, done(b, i, ("split", *e[1:]), SPLITS))
                    for k in range(FT * (kind == "f2"), FT * (1 + (kind == "f2"))):
                        part, ft = divmod(k, FT)
                        ins = pe.matmul(bank[:, 0:DIM], h_parts_of(b, t)[:, part, ft * P:(ft + 1) * P],
                                        w2T[:, ft, :], start=(k == 0), stop=(k == 2 * FT - 1))
                if kind not in HALF_JOBS:
                    ins.then_inc(side_filled, 1)

            def done(b, i, event, count=SIDE):
                k = PLANS[kind_of(b)].index(event)
                assert k < i
                return count.before(b, k + 1)

            def last_before(b, i, name):
                events = PLANS[kind_of(b)]
                return SIDE.before(b, max(k for k in range(i) if events[k][0] == name) + 1)

            def prep_done(b, i, u):
                events = PLANS[kind_of(b)]
                return SIDE.before(b, max(k for k in range(i) if events[k][0] in ("prep_q", "prep_k")) + 1)

            def xt_done(b, i, e, events):
                if events is not None:
                    last = max(k for k in range(i) if events[k][0] in ("xt", "w_qkv"))
                    return counted(events[:last + 1], SIDE.weigh)
                return last_before(b, i, "xt")

            for i, e in enumerate(PROLOGUE):
                local = counted(PROLOGUE[:i], SIDE.weigh)
                if e[0] == "scores":
                    pe.wait_ge(side_drained, local)
                    scores_step(0, 0, 0)
                elif e[0] in SIDE_JOBS:
                    emit(0, i, e, events=PROLOGUE, local=local)
            batches(pe, emit)

        @block.vector
        def _(dve):
            links = [0]

            def link(ins, wait=dve.wait_ge):
                links[0] += 1
                ins.then_inc(linked, 1)
                wait(linked, link_base[0] + links[0])

            link_base = [0]

            def squares(b, pair, ahead):
                flat = qk_raw[:, :, :].rearrange("p t c -> p (t c)")
                n = PAIRS * (b + ahead) + pair
                if not (isinstance(n, int) and n == 0):
                    dve.wait_ge(parts_ready, n)
                link(dve.tensor_tensor(qk_norm[:, :, :].rearrange("p t c -> p (t c)"), flat, flat, ALU.mult))
                sum_squares(qk_norm)

            def sum_squares(squared):
                link(dve.tensor_reduce(ssq[:, :], squared[:, :, :].rearrange("p t (h d) -> p (t h) d", d=HEAD_DIM),
                                       AX.X, ALU.add))

            def times_rms(dst, src):
                return dve.tensor_tensor(dst[:, :, :].rearrange("p t (h d) -> p (t h) d", d=HEAD_DIM),
                                         src[:, :, :].rearrange("p t (h d) -> p (t h) d", d=HEAD_DIM),
                                         rms[:, 1, :].unsqueeze(2).to_broadcast([P, 64, HEAD_DIM]), ALU.mult)

            def inverse_rms():
                link(dve.tensor_scalar(ssq[:, :], ssq[:, :], 1.0 / HEAD_DIM, RMS_EPS, ALU.mult, ALU.add))
                link(dve.tensor_scalar(rms[:, 0, :].bitcast(INT32), ssq[:, :].bitcast(INT32), -0.5, float(0x5F3759DF),
                                       ALU.mult, ALU.add))
                for k in range(2):
                    newton_step(k)

            def newton_step(k):
                y, y2 = rms[:, k % 2, :], rms[:, (k + 1) % 2, :]
                link(dve.tensor_tensor(newton[:, :], y, y, ALU.mult))
                link(dve.scalar_tensor_tensor(newton[:, :], newton[:, :], -0.5, ssq[:, :], op0=ALU.mult,
                                              op1=ALU.mult))
                link(dve.scalar_tensor_tensor(y2, newton[:, :], 1.5, y, op0=ALU.add, op1=ALU.mult))

            def normalise(b, pair, ahead):
                newton_step(2)
                link(times_rms(qk_norm, qk_raw))
                for t in range(2):
                    for which in range(2):
                        high, _ = part_slots(b + ahead, 2 * pair + t, which)
                        ins = dve.tensor_copy(high, head_view(t, which))
                ins.then_inc(high_ready, 1)

            def statistics(k, src):
                link(dve.bn_stats(stats[:, :], src), wait=lambda *x: hold(dve, *x))
                link(dve.bn_aggr(mean_var[:, k, :], stats[:, :]))
                dve.tensor_scalar(var_eps[:, k:k + 1], mean_var[:, k, 1:2], LN_EPS, None, ALU.add)\
                    .then_inc(var_ready, 1)

            def layernorm(k, src, dst):
                return dve.tensor_scalar(dst, src, mean_var[:, k, 0:1], inv_std[:, k:k + 1], ALU.subtract, ALU.mult)

            def emit(b, i, e, n=None, local=None, base=None):
                kind = e[0]
                if base is None:
                    base = LINK.before(b, i)
                link_base[0], links[0] = base, 0
                if kind == "norm0":
                    squares(b, e[1], e[2])
                elif kind == "norm1":
                    inverse_rms()
                elif kind == "norm2":
                    normalise(b, e[1], e[2])
                elif kind == "ln1":
                    _, half, t, back = e
                    dve.wait_ge(inv_std_ready, last_ln(b, i, "wo"))
                    w = ADDS.before(b, i)
                    if not (isinstance(w, int) and w == 0):
                        dve.wait_ge(x1_b2_ready, w)
                    link(layernorm(0, z[:, 0, :], x1[:, t % 2, :]))
                    link(dve.tensor_copy(x1_parts[:, t % 2, 0, :], x1[:, t % 2, :]))
                    dve.tensor_tensor(x1_parts[:, t % 2, 1, :], x1[:, t % 2, :], x1_parts[:, t % 2, 0, :],
                                      ALU.subtract).then_inc(x1_ready, 1)
                elif kind == "ln2":
                    t = e[2]
                    dve.wait_ge(inv_std_ready, last_ln(b, i, "f2"))
                    dve.wait_ge(y_out_free[t % 2], stored_before(b, i, t) + 16)
                    layernorm(1, z[:, 1 + t % 2, :], y_out[:, t % 2, :]).then_inc(out_ready, 1)
                elif kind == "copy":
                    u = e[1]
                    dve.wait_ge(attend_done, step_index(b + e[2], u, 0) + UNIT_STEPS[unit_half(u)])
                    dve.tensor_copy(yT_unit[:, :], attended[:, :]).then_inc(yT_copied, 1)
                elif kind == "split":
                    _, half, t, back = e
                    dve.wait_ge(gelu_done, GELUS.before(b, i))
                    dve.wait_ge(side_filled, SIDE.before(b, i))
                    h = hidden[:, t].rearrange("p f c -> p (f c)")
                    parts = h_parts_of(b, t)
                    link(dve.tensor_scalar(parts[:, 0, :], h, h_scale[:, 4:5], None, ALU.mult))
                    dve.scalar_tensor_tensor(parts[:, 1, :], h, h_scale[:, 4:5], parts[:, 0, :],
                                             op0=ALU.mult, op1=ALU.subtract).then_inc(h_split, 1)
                elif kind == "h_sum":
                    dve.wait_ge(b1_loaded, 16)
                    dve.tensor_reduce(h_scale[:, 0:1], b1_col[:, :], AX.X, ALU.max,
                                      apply_absolute_value=True).then_inc(summed, 1)
                elif kind == "t_sum":
                    dve.wait_ge((w1_loaded, w2_loaded)[e[1]], 16)
                    dve.tensor_reduce(tern[:, e[1], 0:1], (w1_in, w2_in)[e[1]].rearrange("p a c -> p (a c)"),
                                      AX.X, ALU.add, apply_absolute_value=True).then_inc(summed, 1)
                elif kind == "t_make":
                    w = e[1]
                    dve.wait_ge(side_drained, SIDE.before(b, i))
                    dve.wait_ge(parts_ready, PAIRS)
                    flat = (w1_in, w2_in)[w].rearrange("p a c -> p (a c)")
                    dst = (w1_tern, w2_tern)[w].rearrange("p a c -> p (a c)")
                    link(dve.tensor_scalar(w_neg, flat, tern[:, w, 3:4], None, ALU.is_lt))
                    dve.scalar_tensor_tensor(dst, flat, tern[:, w, 2:3], w_neg, op0=ALU.is_gt,
                                             op1=ALU.subtract).then_inc(summed, 1)
                if kind not in SIDE_JOBS:
                    return
                if n is None:
                    n = SIDE.before(b, i)
                    local = counted(PLANS[kind_of(b)][:i], SIDE.weigh)
                bank = side[local % SIDE_BANKS]
                bank16 = bank[:, :].bitcast(FP16)
                dve.wait_ge(side_filled, n + 1)
                if kind == "w_qkv":
                    w = e[1]
                    dve.tensor_copy(w_qkvT[:, :, w * DIM:(w + 1) * DIM],
                                    bank[:, :].rearrange("p (k c) -> p k c", k=KT)).then_inc(side_drained, 1)
                elif kind == "w_o":
                    dve.tensor_copy(w_oT[:, :, :].rearrange("p k c -> p (k c)"), bank[:, :])\
                        .then_inc(side_drained, 1)
                elif kind == "b2":
                    dve.tensor_copy(b2_all[:, :], bank[:, 0:DIM]).then_inc(side_drained, 1)
                elif kind == "h_scale":
                    link(dve.tensor_scalar(h_scale[:, 1:2], bank[:, 0:1], float(DIM + 1), None, ALU.add))
                    link(dve.reciprocal(h_scale[:, 2:3], h_scale[:, 1:2]))
                    link(dve.tensor_scalar(h_scale[:, 4:5], h_scale[:, 2:3], 60000.0, 1.0, ALU.mult, ALU.min))
                    link(dve.reciprocal(h_scale[:, 5:6], h_scale[:, 4:5]))
                    dve.sem_inc(side_drained, 1)
                elif kind == "t_mean":
                    m = tern[:, e[1], :]
                    link(dve.tensor_scalar(m[:, 1:2], bank[:, 0:1], 1.0 / (FF * DIM), 1e-8, ALU.mult, ALU.max))
                    dve.tensor_scalar(m[:, 2:3], m[:, 1:2], 0.5, None, ALU.mult)
                    dve.tensor_scalar(m[:, 3:4], m[:, 1:2], -0.5, None, ALU.mult).then_inc(side_drained, 1)
                elif kind == "w1":
                    dve.tensor_copy(w1T[:, e[1], :], bank16).then_inc(side_drained, 1)
                elif kind == "w2":
                    dve.tensor_copy(w2T[:, FT // 2 * e[1]:FT // 2 * (e[1] + 1), :].rearrange("p f c -> p (f c)"),
                                    bank16).then_inc(side_drained, 1)
                elif kind == "fin":
                    u = e[1]
                    hg = u % HGS
                    view = bank[:, :].rearrange("p (t h d) -> p t h d", t=CT, h=GROUP_HEADS)
                    link(dve.reciprocal(inv_den[:, :].rearrange("p (t h) -> p t h", t=CT), view[:, :, :, HEAD_DIM]))
                    dst = y_tok[:, unit_half(u)].rearrange("p t (h d) -> p t h d", d=HEAD_DIM)
                    dve.tensor_tensor(dst[:, :, GROUP_HEADS * hg:GROUP_HEADS * (hg + 1), :],
                                      view[:, :, :, 0:HEAD_DIM],
                                      inv_den[:, :].rearrange("p (t h) -> p t h", t=CT).unsqueeze(3)
                                      .to_broadcast([P, CT, GROUP_HEADS, HEAD_DIM]), ALU.mult)\
                        .then_inc(side_drained, 1)
                elif kind == "prep_q":
                    dve.tensor_copy(qT[:, e[1] % 2].rearrange("p h c -> p (h c)"), bank16).then_inc(side_drained, 1)
                elif kind == "prep_k":
                    dve.tensor_copy(kT[:, e[1] % 2, e[2]].rearrange("p h c -> p (h c)"), bank16)\
                        .then_inc(side_drained, 1)
                elif kind == "xt":
                    dve.tensor_copy(xT[:, e[3]].rearrange("p k c -> p (k c)"), bank[:, 0:DIM])\
                        .then_inc(side_drained, 1)
                elif kind == "qk":
                    dve.tensor_copy(qk_raw[:, e[3], :], bank[:, :]).then_inc(side_drained, 1)
                    dve.wait_ge(side_drained, n + 1)
                elif kind == "v":
                    dve.tensor_copy(values[:, kept_at(b + e[2], 2 * e[1] + e[3], 1), :]
                                    .rearrange("p a c -> p (a c)"), bank[:, 0:DIM]).then_inc(side_drained, 1)
                elif kind == "yt":
                    dve.tensor_copy(yT[:, e[2] % 2].rearrange("p k c -> p (k c)"), bank[:, 0:DIM])\
                        .then_inc(side_drained, 1)
                elif kind == "wo":
                    _, half, t, back = e
                    bb = b + back
                    dve.wait_ge(res_loaded[t % 2], (bb * (TILES // 2) + (CT * half + t) // 2 + 1) * 16)
                    dve.tensor_tensor(z[:, 0, :], bank[:, 0:DIM], x_res[:, t % 2, :], ALU.add)\
                        .then_inc(side_drained, 1)
                    dve.wait_ge(side_drained, n + 1)
                    statistics(0, z[:, 0, :])
                elif kind == "x1t":
                    dve.tensor_copy(x1T[:, e[2] % 2].rearrange("p a k c -> p (a k c)"), bank16[:, 0:2 * DIM])\
                        .then_inc(side_drained, 1)
                elif kind == "f1":
                    _, half, t, back, a = e
                    fs = slice(FT // 2 * a, FT // 2 * (a + 1))
                    dve.tensor_tensor(hidden[:, t, fs, :], bank[:, :].rearrange("p (f t) -> p f t", t=P),
                                      b1_col[:, fs].unsqueeze(2).to_broadcast([P, FT // 2, P]), ALU.add)\
                        .then_inc(side_drained, 1)
                elif kind == "f2":
                    _, half, t, back = e
                    dve.scalar_tensor_tensor(z[:, 1 + t % 2, :], bank[:, 0:DIM], h_scale[:, 5:6],
                                             x1_b2[:, t, :], op0=ALU.mult, op1=ALU.add)\
                        .then_inc(side_drained, 1)
                    dve.wait_ge(side_drained, n + 1)
                    statistics(1, z[:, 1 + t % 2, :])
                assert links[0] == LINKS.get(kind, 0), (kind, links[0])

            def last_ln(b, i, name):
                events = PLANS[kind_of(b)]
                return LN.before(b, max(k for k in range(i) if events[k][0] == name) + 1)

            def stored_before(b, i, t):
                c = Count(lambda e: 16 * int(e[0] == "ln2" and e[2] % 2 == t % 2))
                return c.before(b, i)

            for p in (0, 1):
                i = PROLOGUE.index(("first_norm", p))
                link_base[0], links[0] = counted(PROLOGUE[:i], LINK.weigh), 0
                dve.wait_ge(side_drained, side_jobs_to(("qk", p, 0, 1)))
                if p:
                    dve.wait_ge(first_normed, p)
                sum_squares(first_norms[p])
                inverse_rms()
                newton_step(2)
                times_rms(first_norms[p], first_raw[p]).then_inc(first_normed, 1)
                assert links[0] == LINKS["first_norm"], links[0]
            dve.wait_ge(first_high, 8)
            for which in range(2):
                high, low = part_slots(0, 3, which)
                ins = dve.tensor_tensor(low, head_view(1, which, first_norms[1]), high, ALU.subtract)
            ins.then_inc(first_low, 1)
            batches(dve, emit)


def parts_needed(half):
    return PAIRS if half else PAIRS // 2


_INS = ["L0_attn_x", "L0_attn_w_q", "L0_attn_w_k", "L0_attn_w_v", "L0_attn_w_o",
        "L0_ffn_W1", "L0_ffn_b1", "L0_ffn_W2", "L0_ffn_b2"]


def kernel(**inputs):
    import numpy as np
    import concourse.bacc as bacc
    from concourse.bass_utils import run_bass_kernel_spmd

    nc = bacc.Bacc("TRN2", target_bir_lowering=False, num_devices=1)
    arrays, args = {}, []
    for name in _INS:
        a = np.ascontiguousarray(inputs[name])
        arrays[f"in_{name}"] = a
        args.append(nc.dram_tensor(f"in_{name}", a.shape, mybir.dt.from_np(a.dtype), kind="ExternalInput").ap())
    args.append(nc.dram_tensor("out", (BATCH, SEQ, DIM), FP32, kind="ExternalOutput").ap())
    build(nc, *args)
    r = run_bass_kernel_spmd(nc, [arrays], core_ids=[0])
    return r.results[0]["out"]
```
